# Optimizing a Trainium2 kernel written in Bass

```python
import numpy as np
import jax
import jax.numpy as jnp

def _softmax(x, axis=-1):
    return jax.nn.softmax(x, axis=axis)

def _gelu(x):
    return jax.nn.gelu(x, approximate=True)

def _silu(x):
    return jax.nn.silu(x)

def _sigmoid(x):
    return jax.nn.sigmoid(x)

def _layernorm(x, axis=-1, eps=1e-05):
    m = jnp.mean(x, axis=axis, keepdims=True)
    v = jnp.var(x, axis=axis, keepdims=True)
    return (x - m) / jnp.sqrt(v + eps)

def _scatter_add(tgt, idx, src, axis=0):
    return tgt.at[idx].add(src)

def _segment_sum(src, seg, n):
    return jax.ops.segment_sum(src, seg, n)
kernel_name = 'mk_adj_preln_d2_adj_r2_82ae85'

def setup_inputs(seed: int=0):
    np.random.seed(seed)
    _w = jnp.asarray

    def _rec_inputs():
        import jax
        import jax.numpy as jnp
        _gk = jax.random.key(seed)
        x = -0.0005207 + 1.001 * jax.random.normal(jax.random.fold_in(_gk, 1), (16, 512, 128), jnp.float32)
        _a = jax.random.bernoulli(jax.random.fold_in(_gk, 2), 0.00390625, (512, 512))
        _a = jnp.logical_or(_a, jnp.swapaxes(_a, -1, -2))
        _a = jnp.logical_or(_a, jnp.eye(512, dtype=bool))
        adj = _a
        return (x, adj)
    x, adj = _rec_inputs()

    def _L0_gnn_setup():
        import jax, jax.numpy as jnp
        import numpy as np
        D_MODEL = 128
        N_HEADS = 8
        D_HEAD = D_MODEL // N_HEADS
        B, G = (4, 1024)
        key = jax.random.key(seed)
        ks = jax.random.split(key, 6)
        x = jax.random.normal(ks[0], (B, G, D_MODEL), dtype=jnp.float32)
        allow = jax.random.randint(ks[1], (G, G), 0, 2).astype(bool)
        allow = allow | jnp.eye(G, dtype=bool)
        s_in = 1.0 / np.sqrt(D_MODEL)
        W_qkv = jax.random.uniform(ks[2], (D_MODEL, 3 * D_MODEL), jnp.float32, -s_in, s_in)
        b_qkv = jax.random.uniform(ks[3], (3 * D_MODEL,), jnp.float32, -s_in, s_in)
        W_out = jax.random.uniform(ks[4], (D_MODEL, D_MODEL), jnp.float32, -s_in, s_in)
        b_out = jax.random.uniform(ks[5], (D_MODEL,), jnp.float32, -s_in, s_in)
        return {'x': x, 'allow_mask_bool': allow, 'W_qkv': W_qkv, 'b_qkv': b_qkv, 'W_out': W_out, 'b_out': b_out}
    _L0_gnn_all = _L0_gnn_setup()
    _L0_gnn_in = {k: v for k, v in _L0_gnn_all.items() if k in ('W_qkv', 'b_qkv', 'W_out', 'b_out')}
    del _L0_gnn_all

    def _L1_gnn_setup():
        import jax, jax.numpy as jnp
        import numpy as np
        T_WAKE = 0.1
        SIGMA_GRAV = 1.0
        EPS = 1e-08
        B, N, D = (2, 2048, 128)

        def _zero_diag(A):
            n = A.shape[-1]
            eye = jnp.eye(n, dtype=A.dtype)
            return A * (1.0 - eye)

        def _cosine_adjacency(z):
            norm = jnp.maximum(jnp.linalg.norm(z, axis=-1, keepdims=True), EPS)
            zn = z / norm
            A = jnp.maximum(jnp.einsum('bnd,bmd->bnm', zn, zn), 0.0)
            return _zero_diag(A)

        def _rbf_adjacency(z, sigma):
            sq = jnp.sum(z * z, axis=-1, keepdims=True)
            d2 = sq + jnp.swapaxes(sq, -1, -2) - 2.0 * jnp.einsum('bnd,bmd->bnm', z, z)
            d2 = jnp.maximum(d2, 0.0)
            A = jnp.exp(-d2 / (2.0 * sigma * sigma))
            return _zero_diag(A)

        def _row_stochastic_causal(A, causal_mask):
            A = A * causal_mask.astype(A.dtype)
            deg = jnp.maximum(jnp.sum(A, axis=-1, keepdims=True), EPS)
            return A / deg
        key = jax.random.key(seed)
        ks = jax.random.split(key, 5)
        s = 1.0 / np.sqrt(D)
        return {'h': jax.random.normal(ks[0], (B, N, D), dtype=jnp.float32), 'causal_mask': jnp.tril(jnp.ones((N, N), dtype=bool)), 'Wl': jax.random.normal(ks[1], (D, D), dtype=jnp.float32) * s, 'Wg': jax.random.normal(ks[2], (D, D), dtype=jnp.float32) * s, 'Wv': jax.random.normal(ks[3], (D, D), dtype=jnp.float32) * s, 'Wo': jax.random.normal(ks[4], (D, D), dtype=jnp.float32) * s}
    _L1_gnn_all = _L1_gnn_setup()
    _L1_gnn_in = {k: v for k, v in _L1_gnn_all.items() if k in ('Wl', 'Wg', 'Wv', 'Wo')}
    del _L1_gnn_all
    return {'x': x, 'adj': adj, 'L0_gnn_W_qkv': _L0_gnn_in['W_qkv'], 'L0_gnn_b_qkv': _L0_gnn_in['b_qkv'], 'L0_gnn_W_out': _L0_gnn_in['W_out'], 'L0_gnn_b_out': _L0_gnn_in['b_out'], 'L1_gnn_Wl': _L1_gnn_in['Wl'], 'L1_gnn_Wg': _L1_gnn_in['Wg'], 'L1_gnn_Wv': _L1_gnn_in['Wv'], 'L1_gnn_Wo': _L1_gnn_in['Wo']}

def reference(x, adj, L0_gnn_W_qkv, L0_gnn_b_qkv, L0_gnn_W_out, L0_gnn_b_out, L1_gnn_Wl, L1_gnn_Wg, L1_gnn_Wv, L1_gnn_Wo):
    import jax
    import jax.numpy as jnp

    def _L0_gnn_ref(x, allow_mask_bool, W_qkv, b_qkv, W_out, b_out):
        import jax, jax.numpy as jnp
        import numpy as np
        D_MODEL = 128
        N_HEADS = 8
        D_HEAD = D_MODEL // N_HEADS
        B, G = (4, 1024)
        Bb, Gg, Dm = x.shape
        h, d = (N_HEADS, D_HEAD)
        qkv = x @ W_qkv + b_qkv
        qkv = qkv.reshape(Bb, Gg, 3, h, d)
        q = qkv[:, :, 0].transpose(0, 2, 1, 3)
        k = qkv[:, :, 1].transpose(0, 2, 1, 3)
        v = qkv[:, :, 2].transpose(0, 2, 1, 3)
        scale = 1.0 / jnp.sqrt(jnp.asarray(d, x.dtype))
        scores = jnp.einsum('bhqd,bhkd->bhqk', q, k) * scale
        neg_inf = jnp.asarray(-jnp.inf, scores.dtype)
        scores = jnp.where(allow_mask_bool[None, None], scores, neg_inf)
        attn = jax.nn.softmax(scores, axis=-1)
        y = jnp.einsum('bhqk,bhkd->bhqd', attn, v)
        y = y.transpose(0, 2, 1, 3).reshape(Bb, Gg, Dm)
        return y @ W_out + b_out

    def _L1_gnn_ref(h, causal_mask, Wl, Wg, Wv, Wo):
        import jax, jax.numpy as jnp
        import numpy as np
        T_WAKE = 0.1
        SIGMA_GRAV = 1.0
        EPS = 1e-08
        B, N, D = (2, 2048, 128)

        def _zero_diag(A):
            n = A.shape[-1]
            eye = jnp.eye(n, dtype=A.dtype)
            return A * (1.0 - eye)

        def _cosine_adjacency(z):
            norm = jnp.maximum(jnp.linalg.norm(z, axis=-1, keepdims=True), EPS)
            zn = z / norm
            A = jnp.maximum(jnp.einsum('bnd,bmd->bnm', zn, zn), 0.0)
            return _zero_diag(A)

        def _rbf_adjacency(z, sigma):
            sq = jnp.sum(z * z, axis=-1, keepdims=True)
            d2 = sq + jnp.swapaxes(sq, -1, -2) - 2.0 * jnp.einsum('bnd,bmd->bnm', z, z)
            d2 = jnp.maximum(d2, 0.0)
            A = jnp.exp(-d2 / (2.0 * sigma * sigma))
            return _zero_diag(A)

        def _row_stochastic_causal(A, causal_mask):
            A = A * causal_mask.astype(A.dtype)
            deg = jnp.maximum(jnp.sum(A, axis=-1, keepdims=True), EPS)
            return A / deg
        z_l = h @ Wl
        z_g = h @ Wg
        v = h @ Wv
        A_l = _cosine_adjacency(z_l)
        A_g = _rbf_adjacency(z_g, SIGMA_GRAV)
        K_l = _row_stochastic_causal(A_l, causal_mask)
        K_g = _row_stochastic_causal(A_g, causal_mask)
        w_l, w_g = (1.0 - T_WAKE, T_WAKE)
        K = w_l * K_l + w_g * K_g
        return jnp.einsum('bnm,bmd->bnd', K, v) @ Wo
    h = jnp.maximum(_layernorm(x, axis=-1), 0.0)
    x = x + _L0_gnn_ref(h, adj, L0_gnn_W_qkv, L0_gnn_b_qkv, L0_gnn_W_out, L0_gnn_b_out)
    h = jnp.maximum(_layernorm(x, axis=-1), 0.0)
    x = x + _L1_gnn_ref(h, adj, L1_gnn_Wl, L1_gnn_Wg, L1_gnn_Wv, L1_gnn_Wo)
    return x

_drawn_inputs = setup_inputs


def setup_inputs(seed=0):
    import zlib

    import numpy as np

    out = dict(_drawn_inputs(seed))
    spreads = {}
    factors = {'L1_gnn_Wg': 8.0}
    for name, (base, spread) in spreads.items():
        noise = np.random.default_rng([zlib.crc32(name.encode()), seed]).standard_normal(out[name].shape)
        drawn = base * np.exp(spread * noise) if base else spread * noise
        out[name] = jnp.asarray(drawn.astype(out[name].dtype))
    for name, factor in factors.items():
        out[name] = (out[name] * factor).astype(out[name].dtype)
    return out
```

```python
from contextlib import ExitStack

import concourse.bass as bass
from concourse import mybir

F32 = mybir.dt.float32
BF16 = mybir.dt.bfloat16
ALU = mybir.AluOpType
ACT = mybir.ActivationFunctionType
AX_X = mybir.AxisListType.X

P = 128
LN_EPS = 1e-5
KERNEL_EPS = 1e-8
W_LOCAL, W_GLOBAL = 0.9, 0.1
BIG = 2.0 ** 100
LEAST_SQUARE = KERNEL_EPS * KERNEL_EPS

Q_PARTS = (0, 0, 0, 1, 1, 2)
K_PARTS = (0, 1, 2, 0, 1, 0)

TURN_LAG = 3
VECTOR_UNITS = (3, 9, 15, 21, 27)
COS_SLOTS, RBF_SLOTS = (0, 2, 8, 10), (1, 3, 9, 11)
PV_PREV_SLOTS, PV_SLOTS = (4, 5, 6, 7), (24, 25, 26, 27)
MIX_SLOTS = (14, 15, 16, 17)
Z_SLOTS = (20, 21, 22, 23)


class Signal:

    def __init__(self, sem, per, step):
        self.sem, self.per, self.step = sem, per, step


def reached(engine, signal, batch, nth=None):
    count = (batch * signal.per + (signal.per if nth is None else nth)) * signal.step
    if isinstance(count, int) and count <= 0:
        return
    engine.wait_ge(signal.sem, count)


def graph_blocks(nc, x, adj, w_qkv, b_qkv, w_out, b_out, w_l, w_g, w_v, w_o, out):
    B, N, D = x.shape
    H = 8
    DH = D // H
    T = N // P
    GROUPS = 2
    HG = H // GROUPS
    SLOTS = H * T
    ROWS = len(Q_PARTS) * DH
    HALF = H // 2
    SCALE = float(DH) ** -0.5
    ZC = 3 * D + 2
    assert D == P and T == 4 and HG * 32 == P

    copied_by_vector = [u for u in range(SLOTS) if u in VECTOR_UNITS]
    copied_by_scalar = [u for u in range(SLOTS) if u not in VECTOR_UNITS]

    with ExitStack() as ctx:
        def sb(name, shape, dt=F32):
            return ctx.enter_context(nc.sbuf_tensor(name, shape, dt))

        def bank(name):
            return ctx.enter_context(nc.psum_tensor(name, [P, 512], F32))

        def signal(name, per=1, step=1):
            return Signal(ctx.enter_context(nc.semaphore(name)), per, step)

        wqkv_sb = sb("wqkv_sb", [P, 3 * D])
        wz_sb = sb("wz_sb", [P, 3 * D])
        wout_sb = sb("wout_sb", [P, D])
        wv_sb = sb("wv_sb", [P, D])
        wo_sb = sb("wo_sb", [P, D])
        wvT_sb = sb("wvT_sb", [P, D])
        bias_q = sb("bias_q", [P, 1])
        bias_k = sb("bias_k", [P, 1])
        bias_v = sb("bias_v", [P, D])
        bias_out = sb("bias_out", [P, D])
        ident = sb("ident", [P, P])
        neg_half = sb("neg_half", [P, P])
        minus_half = sb("minus_half", [P, T])
        degree_floor = sb("degree_floor", [P, 2])
        adj_sb = sb("adj_sb", [P, T, N], adj.dtype)
        mask_add = sb("mask_add", [P, T, N], BF16)
        mask_t = sb("mask_t", [P, T, N], BF16)

        x_sb = sb("x_sb", [P, T, D])
        bn_sb = sb("bn_sb", [P, T, 6])
        moments = sb("moments", [P, T, 2])
        var_eps = sb("var_eps", [P, T])
        rstd = sb("rstd", [P, T])
        x_norm = sb("x_norm", [P, T, D])
        x_biased = sb("x_biased", [P, T, D])
        x_resid = sb("x_resid", [P, T, D])
        hT = sb("hT", [P, N])
        split = sb("split", [P, 2, 3, N], BF16)
        resid = sb("resid", [P, 2, N])
        qk_rows = sb("qk_rows", [ROWS, 2, H, N], BF16)
        v_cols = sb("v_cols", [P, T, H, 32])
        masked = sb("masked", [P, 4, N])
        neg_max = sb("neg_max", [P, SLOTS])
        probs = sb("probs", [P, 4, N])
        probs_t = sb("probs_t", [P, GROUPS, HG, T, N])
        pv_sb = sb("pv_sb", [P, N])
        inv_den = sb("inv_den", [P, T, HG])
        y_sb = sb("y_sb", [P, T, D])
        yT = sb("yT", [P, N])

        x1 = sb("x1", [P, T, D])
        x1_kept = sb("x1_kept", [P, T, D])
        bn2_sb = sb("bn2_sb", [P, T, 6])
        moments2 = sb("moments2", [P, T, 2])
        var_eps2 = sb("var_eps2", [P, T])
        rstd2 = sb("rstd2", [P, T])
        x1_norm = sb("x1_norm", [P, T, D])
        h2T = sb("h2T", [P, N])
        z = sb("z", [P, T, ZC])
        z_square = sb("z_square", [P, T, 2 * D])
        square_sum = sb("square_sum", [P, T, 2])
        norm_floor = sb("norm_floor", [P, T])
        inv_norm = sb("inv_norm", [P, T])
        rbf_bias = sb("rbf_bias", [P, T])
        zl_unit = sb("zl_unit", [P, T, D])
        zlT = sb("zlT", [P, N])
        zgT = sb("zgT", [P, N])
        zgT_square = sb("zgT_square", [P, N])
        col_term = sb("col_term", [P, N])
        rbf_arg = sb("rbf_arg", [P, 2, N])
        rbf_exp = sb("rbf_exp", [P, 2, N])
        adj_cos = sb("adj_cos", [P, T, N])
        adj_rbf = sb("adj_rbf", [P, T, N])
        degree = sb("degree", [P, 2])
        inv_degree = sb("inv_degree", [P, 2])
        half_sum = sb("half_sum", [P, D])
        out_sb = sb("out_sb", [P, T, D])

        split_dram = nc.dram_tensor("split_dram", (2, 3, P, N), BF16, kind="Internal").ap()

        score_bank = [bank("score0"), bank("score1")]
        turn_bank = [bank("turn0"), bank("turn1")]
        pv_bank = bank("pv")
        work_bank = bank("work")
        adj_bank = [bank("adj0"), bank("adj1")]

        s_loaded = signal("setup_loaded", 12, 16)
        s_consts = signal("setup_consts")
        s_ident = signal("setup_ident", 2)
        s_zeroed = signal("setup_zeroed")
        s_adj_cast = signal("setup_adj_cast")
        s_adj_open = signal("setup_adj_open")
        s_adj_turned = signal("setup_adj_turned", T)
        s_mask_add = signal("setup_mask_add")
        s_masks = signal("setup_masks")
        s_wv_turned = signal("setup_wv_turned")
        s_wv_copied = signal("setup_wv_copied")
        s_wvo = signal("setup_wvo")
        s_wvo_copied = signal("setup_wvo_copied")

        dve_steps = signal("dve_steps")
        pool_steps = signal("pool_steps")

        x_loaded = signal("x_loaded", 1, 16)
        ln_bn = signal("ln_bn")
        ln_moments = signal("ln_moments")
        ln_var = signal("ln_var")
        ln_rstd = signal("ln_rstd")
        ln_done = signal("ln_done")
        x_biased_ready = signal("x_biased_ready")
        x_resid_ready = signal("x_resid_ready")
        hT_filled = signal("hT_filled")
        hT_ready = signal("hT_ready")
        qk_filled = signal("qk_filled", 2)
        hi_ready = signal("hi_ready", 2)
        rest_ready = signal("rest_ready", 2)
        mid_ready = signal("mid_ready", 2)
        lo_ready = signal("lo_ready", 2)
        split_stored = signal("split_stored", 2, 16)
        rows_loaded = [signal(f"rows_loaded{h}", 2 * len(Q_PARTS), 16) for h in range(2)]

        v_filled = signal("v_filled")
        v_ready = signal("v_ready")
        scores_filled = signal("scores_filled", SLOTS)
        masked_ready = signal("masked_ready", SLOTS)
        probs_ready = signal("probs_ready", SLOTS)
        turned = signal("turned", SLOTS)
        copied_vector = signal("copied_vector", len(copied_by_vector))
        copied_scalar = signal("copied_scalar", len(copied_by_scalar))
        pv_filled = signal("pv_filled", GROUPS)
        pv_copied = signal("pv_copied", GROUPS)
        y_turned = signal("y_turned", GROUPS)
        den_ready = signal("den_ready", GROUPS)
        y_ready = signal("y_ready", GROUPS)
        yT_filled = signal("yT_filled")
        yT_ready = signal("yT_ready")
        attn_filled = signal("attn_filled")
        x1_ready = signal("x1_ready")
        x1_kept_ready = signal("x1_kept_ready")

        ln2_bn = signal("ln2_bn")
        ln2_moments = signal("ln2_moments")
        ln2_var = signal("ln2_var")
        ln2_rstd = signal("ln2_rstd")
        ln2_done = signal("ln2_done")
        h2T_filled = signal("h2T_filled")
        h2T_ready = signal("h2T_ready")
        z_filled = signal("z_filled", T)
        z_ready = signal("z_ready", T)
        z_squared = signal("z_squared")
        sums_ready = signal("sums_ready")
        floor_ready = signal("floor_ready")
        rbf_bias_ready = signal("rbf_bias_ready")
        inv_norm_ready = signal("inv_norm_ready")
        unit_ready = signal("unit_ready")
        zgT_filled = signal("zgT_filled")
        zgT_ready = signal("zgT_ready")
        zgT_squared = signal("zgT_squared")
        col_filled = signal("col_filled")
        col_ready = signal("col_ready")
        zlT_filled = signal("zlT_filled")
        zlT_ready = signal("zlT_ready")
        cos_filled = signal("cos_filled", T)
        cos_ready = signal("cos_ready", T)
        rbf_filled = signal("rbf_filled", T)
        rbf_arg_ready = signal("rbf_arg_ready", T)
        rbf_exp_ready = signal("rbf_exp_ready", T)
        rbf_ready = signal("rbf_ready", T)
        mix_filled = signal("mix_filled", T)
        degree_ready = signal("degree_ready", T)
        inv_degree_ready = signal("inv_degree_ready", T)
        half_ready = signal("half_ready", T)
        out_ready = signal("out_ready", T)
        out_stored = signal("out_stored", 1, 16)

        def step_over(engine, counter):
            engine.sem_inc(counter.sem, 1)

        def lagged(i, slot, lag):
            return (i, slot - lag) if slot >= lag else (i - 1, slot - lag + SLOTS)

        def copies_reached(engine, batch, last):
            by_vector = sum(u <= last for u in copied_by_vector)
            by_scalar = sum(u <= last for u in copied_by_scalar)
            if by_vector:
                reached(engine, copied_vector, batch, by_vector)
            if by_scalar:
                reached(engine, copied_scalar, batch, by_scalar)

        def iterations(engine, body):
            for i in (-1, 0, 1, 2):
                body(i, i + 1 < B, 0 <= i, 1 <= i, 2 <= i)
            with engine.Fori(3, B - 1) as i:
                body(i, True, True, True, True)
            for i in (B - 1, B, B + 1):
                body(i, False, i < B, i - 1 < B, True)

        WORK_USES = (
            [("v", v_ready, 1, 0), ("y1", y_ready, 2, -1), ("hT", hT_ready, 1, 1), ("yT", yT_ready, 1, -1),
             ("q", rest_ready, 1, 1), ("attn", x1_ready, 1, -1), ("k", rest_ready, 2, 1), ("h2T", h2T_ready, 1, -1)]
            + [(f"z{t}", z_ready, t + 1, -1) for t in range(T)]
            + [("zgT", zgT_squared, 1, -1), ("col", col_ready, 1, -1), ("y0", y_ready, 1, 0),
               ("zlT", zlT_ready, 1, -1)]
        )

        def work_bank_free(engine, i, use):
            at = [name for name, _, _, _ in WORK_USES].index(use)
            for back in range(1, len(WORK_USES) + 1):
                _, sig, nth, offset = WORK_USES[(at - back) % len(WORK_USES)]
                batch = i + offset - (1 if back > at else 0)
                if isinstance(batch, int) and not 0 <= batch < B:
                    continue
                reached(engine, sig, batch, nth)
                return

        block = ctx.enter_context(nc.Block())

        @block.sync
        def _(sp):
            for dst, src in (
                (adj_sb[:, :, :], adj.rearrange("(t p) k -> p t k", p=P)),
                (wqkv_sb[:, :], w_qkv),
                (wout_sb[:, :], w_out),
                (wz_sb[:, 0:D], w_l),
                (wz_sb[:, D:2 * D], w_g),
                (wv_sb[:, :], w_v),
                (wo_sb[:, :], w_o),
                (bias_q[:, :], b_qkv[0:D].rearrange("(p o) -> p o", o=1)),
                (bias_k[:, :], b_qkv[D:2 * D].rearrange("(p o) -> p o", o=1)),
                (bias_v[:, :], b_qkv[2 * D:3 * D].partition_broadcast(P)),
                (bias_out[:, :], b_out.partition_broadcast(P)),
            ):
                sp.dma_start(dst, src).then_inc(s_loaded.sem, 16)

            def load_x(batch):
                sp.dma_start(x_sb[:, :, :], x[batch].rearrange("(t p) d -> p t d", p=P)).then_inc(x_loaded.sem, 16)

            def load_rows(batch, half):
                h0 = half * HALF
                for which, parts in enumerate((Q_PARTS, K_PARTS)):
                    for block_row, part in enumerate(parts):
                        src = split_dram[which, part, h0 * DH:(h0 + HALF) * DH, :]
                        sp.dma_start(qk_rows[block_row * DH:(block_row + 1) * DH, which, h0:h0 + HALF, :],
                                     src.rearrange("(h f) n -> f h n", f=DH)).then_inc(rows_loaded[half].sem, 16)

            def body(i, ahead, att, prev, old):
                if ahead:
                    reached(sp, ln_done, i)
                    reached(sp, x_biased_ready, i)
                    load_x(i + 1)
                    reached(sp, rows_loaded[0], i)
                    reached(sp, rows_loaded[1], i)
                    for which in range(2):
                        reached(sp, lo_ready, i + 1, which + 1)
                        reached(sp, hi_ready, i + 1, which + 1)
                        sp.dma_start(split_dram[which].rearrange("c f n -> f c n"),
                                     split[:, which, :, :]).then_inc(split_stored.sem, 16)
                    reached(sp, split_stored, i + 1)
                    reached(sp, scores_filled, i, SLOTS // 2)
                    load_rows(i + 1, 0)
                if old:
                    reached(sp, out_ready, i - 2)
                    sp.dma_start(out[i - 2].rearrange("(t p) d -> p t d", p=P),
                                 out_sb[:, :, :]).then_inc(out_stored.sem, 16)
                if ahead:
                    reached(sp, scores_filled, i, SLOTS)
                    load_rows(i + 1, 1)

            iterations(sp, body)
            reached(sp, out_stored, B - 1)
            reached(sp, split_stored, B - 1)

        @block.gpsimd
        def _(pool):
            pool.memset(ident[:, :], 0.0)
            pool.memset(neg_half[:, :], -0.5)
            pool.memset(minus_half[:, :], -0.5)
            pool.memset(degree_floor[:, 0:1], KERNEL_EPS / W_LOCAL)
            pool.memset(degree_floor[:, 1:2], KERNEL_EPS / W_GLOBAL)
            pool.memset(z[:, :, 3 * D:3 * D + 1], 1.0 / W_LOCAL)
            pool.memset(z[:, :, 3 * D + 1:ZC], 1.0 / W_GLOBAL)
            pool.memset(v_cols[:, :, :, DH + 1:32], 0.0)
            pool.memset(v_cols[:, :, :, DH:DH + 1], 1.0).then_inc(s_consts.sem, 1)
            pool.wait_ge(s_consts.sem, 1)
            pool.affine_select(out=ident[:, :], in_=ident[:, :], compare_op=ALU.not_equal, fill=1.0, base=0,
                               pattern=[[-1, P]], channel_multiplier=1).then_inc(s_ident.sem, 1)
            pool.wait_ge(s_adj_cast.sem, 1)
            pool.affine_select(out=probs[:, :, :], in_=probs[:, :, :], compare_op=ALU.not_equal, fill=0.0,
                               base=0, pattern=[[P, T], [-1, N]],
                               channel_multiplier=1).then_inc(s_adj_open.sem, 1)
            pool.wait_ge(s_loaded.sem, 11 * 16)

            def body(i, ahead, att, prev, old):
                for slot in range(SLOTS):
                    if slot == 7 and ahead:
                        reached(pool, ln_moments, i + 1)
                        reached(pool, ln_done, i)
                        step_over(pool, pool_steps)
                        pool.tensor_scalar(var_eps[:, :], moments[:, :, 1], LN_EPS, None,
                                           ALU.add).then_inc(ln_var.sem, 1)
                        reached(pool, ln_var, i + 1)
                        pool.tensor_tensor(rstd[:, :], var_eps[:, :], minus_half[:, :],
                                           ALU.pow).then_inc(ln_rstd.sem, 1)
                    if slot in (14, 16) and ahead:
                        which = (slot - 14) // 2
                        reached(pool, split_stored, i, which + 1)
                        reached(pool, rest_ready, i + 1, which + 1)
                        step_over(pool, pool_steps)
                        pool.tensor_copy(split[:, which, 1, :], resid[:, which, :]).then_inc(mid_ready.sem, 1)
                        reached(pool, mid_ready, i + 1, which + 1)
                        pool.tensor_tensor(split[:, which, 2, :], resid[:, which, :], split[:, which, 1, :],
                                           ALU.subtract).then_inc(lo_ready.sem, 1)
                    if slot == 17 and prev:
                        reached(pool, ln2_moments, i - 1)
                        reached(pool, ln2_done, i - 2)
                        step_over(pool, pool_steps)
                        pool.tensor_scalar(var_eps2[:, :], moments2[:, :, 1], LN_EPS, None,
                                           ALU.add).then_inc(ln2_var.sem, 1)
                        reached(pool, ln2_var, i - 1)
                        pool.tensor_tensor(rstd2[:, :], var_eps2[:, :], minus_half[:, :],
                                           ALU.pow).then_inc(ln2_rstd.sem, 1)
                    if slot == 18 and att:
                        reached(pool, x1_ready, i - 1)
                        reached(pool, x_biased_ready, i)
                        step_over(pool, pool_steps)
                        pool.tensor_copy(x_resid[:, :, :], x_biased[:, :, :]).then_inc(x_resid_ready.sem, 1)
                    if slot == 19 and ahead:
                        reached(pool, x_loaded, i + 1)
                        reached(pool, x_resid_ready, i)
                        pool.tensor_tensor(x_biased[:, :, :], x_sb[:, :, :],
                                           bias_out[:, :].unsqueeze(1).broadcast_to([P, T, D]),
                                           ALU.add).then_inc(x_biased_ready.sem, 1)
                    if slot == 20 and prev:
                        reached(pool, x1_ready, i - 1)
                        reached(pool, out_ready, i - 2)
                        step_over(pool, pool_steps)
                        pool.tensor_copy(x1_kept[:, :, :], x1[:, :, :]).then_inc(x1_kept_ready.sem, 1)
                    if slot == 24 and prev:
                        reached(pool, z_ready, i - 1)
                        reached(pool, sums_ready, i - 2)
                        pool.tensor_tensor(z_square[:, :, :], z[:, :, 0:2 * D], z[:, :, 0:2 * D],
                                           ALU.mult).then_inc(z_squared.sem, 1)
                    if slot == 26 and prev:
                        reached(pool, sums_ready, i - 1)
                        step_over(pool, pool_steps)
                        pool.tensor_scalar(norm_floor[:, :], square_sum[:, :, 0], LEAST_SQUARE, None,
                                           ALU.max).then_inc(floor_ready.sem, 1)
                        reached(pool, rbf_exp_ready, i - 2)
                        step_over(pool, pool_steps)
                        pool.tensor_scalar(rbf_bias[:, :], square_sum[:, :, 1], -0.5, None,
                                           ALU.mult).then_inc(rbf_bias_ready.sem, 1)
                        reached(pool, floor_ready, i - 1)
                        pool.tensor_tensor(inv_norm[:, :], norm_floor[:, :], minus_half[:, :],
                                           ALU.pow).then_inc(inv_norm_ready.sem, 1)
                        reached(pool, inv_norm_ready, i - 1)
                        reached(pool, zlT_filled, i - 2)
                        pool.tensor_tensor(zl_unit[:, :, :], z[:, :, 0:D],
                                           inv_norm[:, :].unsqueeze(2).broadcast_to([P, T, D]),
                                           ALU.mult).then_inc(unit_ready.sem, 1)

            iterations(pool, body)

        @block.tensor
        def _(pe):
            pe.wait_ge(s_ident.sem, 1)
            pe.wait_ge(s_loaded.sem, 11 * 16)
            pe.transpose(adj_bank[0][:, 0:D], wv_sb[:, :], ident[:, :]).then_inc(s_wv_turned.sem, 1)
            pe.wait_ge(s_wv_copied.sem, 1)
            pe.matmul(adj_bank[1][:, 0:D], wvT_sb[:, :], wo_sb[:, :], start=True,
                      stop=True).then_inc(s_wvo.sem, 1)
            pe.wait_ge(s_adj_open.sem, 1)
            for m, dst in enumerate(score_bank + turn_bank):
                for t in range(T):
                    last = pe.transpose(dst[:, t * P:(t + 1) * P], probs[:, t, m * P:(m + 1) * P], ident[:, :])
                last.then_inc(s_adj_turned.sem, 1)
            pe.wait_ge(s_masks.sem, 1)
            pe.wait_ge(s_wvo_copied.sem, 1)

            def scores(batch, u):
                h, t = divmod(u, T)
                if u % (SLOTS // 2) == 0:
                    reached(pe, rows_loaded[u // (SLOTS // 2)], batch)
                reached(pe, masked_ready, batch, u - 1)
                pe.matmul(score_bank[u % 2][:, :], qk_rows[:, 0, h, t * P:(t + 1) * P], qk_rows[:, 1, h, :],
                          start=True, stop=True).then_inc(scores_filled.sem, 1)

            def turn(batch, u):
                reached(pe, probs_ready, batch, u + 1)
                if u >= 2:
                    copies_reached(pe, batch, u - 2)
                else:
                    copies_reached(pe, batch - 1, SLOTS + u - 2)
                for j in range(T):
                    last = pe.transpose(turn_bank[u % 2][:, j * P:(j + 1) * P],
                                        probs[:, u % 4, j * P:(j + 1) * P], ident[:, :])
                last.then_inc(turned.sem, 1)

            def attend(batch, group, j):
                if j == 0:
                    copies_reached(pe, batch, (group + 1) * SLOTS // GROUPS - 1)
                    reached(pe, v_ready, batch)
                    reached(pe, pv_copied, batch, group)
                for hl in range(HG):
                    last = pe.matmul(pv_bank[32 * hl:32 * (hl + 1), :], v_cols[:, j, group * HG + hl, :],
                                     probs_t[:, group, hl, j, :], start=(j == 0), stop=(j == T - 1),
                                     tile_position=(0, 32 * hl))
                if j == T - 1:
                    last.then_inc(pv_filled.sem, 1)

            def turn_tiles(src, ready):
                for t in range(T):
                    last = pe.transpose(work_bank[:, t * P:(t + 1) * P], src(t), ident[:, :])
                last.then_inc(ready.sem, 1)

            def body(i, ahead, att, prev, old):
                for slot in range(SLOTS):
                    if att:
                        scores(i, slot)
                    batch, u = lagged(i, slot, TURN_LAG)
                    if (att if slot >= TURN_LAG else prev):
                        turn(batch, u)

                    if slot in COS_SLOTS and old:
                        m = COS_SLOTS.index(slot)
                        if m == 0:
                            reached(pe, zlT_ready, i - 2)
                            reached(pe, out_ready, i - 3)
                        else:
                            reached(pe, cos_ready, i - 2, m)
                        pe.matmul(adj_bank[0][:, :], zlT[:, m * P:(m + 1) * P], zlT[:, :], start=True,
                                  stop=True).then_inc(cos_filled.sem, 1)
                    if slot in RBF_SLOTS and old:
                        m = RBF_SLOTS.index(slot)
                        if m == 0:
                            reached(pe, zgT_ready, i - 2)
                            reached(pe, out_ready, i - 3)
                        else:
                            reached(pe, rbf_arg_ready, i - 2, m)
                        pe.matmul(adj_bank[1][:, :], zgT[:, m * P:(m + 1) * P], zgT[:, :], start=True,
                                  stop=True).then_inc(rbf_filled.sem, 1)
                    if slot in MIX_SLOTS and old:
                        n = MIX_SLOTS.index(slot)
                        if n == 0:
                            reached(pe, cos_ready, i - 2)
                            reached(pe, rbf_ready, i - 2)
                        elif n >= 2:
                            reached(pe, out_ready, i - 2, n - 1)
                        for at, adjacency in ((0, adj_cos), (256, adj_rbf)):
                            for m in range(T):
                                last = pe.matmul(adj_bank[n % 2][:, at:at + D + 2],
                                                 adjacency[:, m, n * P:(n + 1) * P], z[:, m, 2 * D:ZC],
                                                 start=(m == 0), stop=(m == T - 1))
                        last.then_inc(mix_filled.sem, 1)

                    if slot in PV_PREV_SLOTS and prev:
                        attend(i - 1, 1, PV_PREV_SLOTS.index(slot))
                    if slot in PV_SLOTS and att:
                        attend(i, 0, PV_SLOTS.index(slot))

                    if slot == 8 and att:
                        reached(pe, hT_ready, i)
                        work_bank_free(pe, i, "v")
                        for t in range(T):
                            last = pe.matmul(work_bank[:, t * P:(t + 1) * P], hT[:, t * P:(t + 1) * P],
                                             wqkv_sb[:, 2 * D:3 * D], start=True, stop=True)
                        last.then_inc(v_filled.sem, 1)
                    if slot == 9 and prev:
                        reached(pe, pv_copied, i - 1, 2)
                        work_bank_free(pe, i, "y1")
                        turn_tiles(lambda t: pv_sb[:, t * P:(t + 1) * P], y_turned)
                    if slot == 10 and ahead:
                        reached(pe, ln_done, i + 1)
                        work_bank_free(pe, i, "hT")
                        turn_tiles(lambda t: x_norm[:, t, :], hT_filled)
                    if slot == 11 and prev:
                        reached(pe, y_ready, i - 1, 2)
                        work_bank_free(pe, i, "yT")
                        turn_tiles(lambda t: y_sb[:, t, :], yT_filled)
                    if slot in (12, 14) and ahead:
                        which = (slot - 12) // 2
                        reached(pe, hT_ready, i + 1)
                        work_bank_free(pe, i, "qk"[which])
                        pe.matmul(work_bank[:, :], wqkv_sb[:, which * D:(which + 1) * D], hT[:, :], start=True,
                                  stop=True).then_inc(qk_filled.sem, 1)
                    if slot == 13 and prev:
                        reached(pe, yT_ready, i - 1)
                        work_bank_free(pe, i, "attn")
                        for t in range(T):
                            last = pe.matmul(work_bank[:, t * P:(t + 1) * P], yT[:, t * P:(t + 1) * P],
                                             wout_sb[:, :], start=True, stop=True)
                        last.then_inc(attn_filled.sem, 1)
                    if slot == 19 and prev:
                        reached(pe, ln2_done, i - 1)
                        work_bank_free(pe, i, "h2T")
                        turn_tiles(lambda t: x1_norm[:, t, :], h2T_filled)
                    if slot in Z_SLOTS and prev:
                        t = Z_SLOTS.index(slot)
                        reached(pe, h2T_ready, i - 1)
                        work_bank_free(pe, i, f"z{t}")
                        pe.matmul(work_bank[:, 0:3 * D], h2T[:, t * P:(t + 1) * P], wz_sb[:, :], start=True,
                                  stop=True).then_inc(z_filled.sem, 1)
                    if slot == 26 and prev:
                        reached(pe, z_ready, i - 1)
                        work_bank_free(pe, i, "zgT")
                        turn_tiles(lambda t: z[:, t, D:2 * D], zgT_filled)
                    if slot == 28 and prev:
                        reached(pe, zgT_squared, i - 1)
                        work_bank_free(pe, i, "col")
                        pe.matmul(work_bank[:, :], neg_half[:, :], zgT_square[:, :], start=True,
                                  stop=True).then_inc(col_filled.sem, 1)
                    if slot == 29 and att:
                        reached(pe, pv_copied, i, 1)
                        work_bank_free(pe, i, "y0")
                        turn_tiles(lambda t: pv_sb[:, t * P:(t + 1) * P], y_turned)
                    if slot == 30 and prev:
                        reached(pe, unit_ready, i - 1)
                        work_bank_free(pe, i, "zlT")
                        turn_tiles(lambda t: zl_unit[:, t, :], zlT_filled)

            iterations(pe, body)

        @block.vector
        def _(dve):
            dve.wait_ge(s_loaded.sem, 11 * 16)
            dve.tensor_copy(probs[:, :, :], adj_sb[:, :, :]).then_inc(s_adj_cast.sem, 1)
            dve.tensor_scalar(mask_add[:, :, :], adj_sb[:, :, :], BIG, -BIG, ALU.mult,
                              ALU.add).then_inc(s_mask_add.sem, 1)
            dve.wait_ge(s_wv_turned.sem, 1)
            dve.tensor_copy(wvT_sb[:, :], adj_bank[0][:, 0:D]).then_inc(s_wv_copied.sem, 1)
            dve.wait_ge(s_wvo.sem, 1)
            dve.tensor_copy(wz_sb[:, 2 * D:3 * D], adj_bank[1][:, 0:D]).then_inc(s_wvo_copied.sem, 1)
            for m, src in enumerate(score_bank + turn_bank):
                dve.wait_ge(s_adj_turned.sem, m + 1)
                last = dve.tensor_copy(mask_t[:, m, :], src[:, :])
            last.then_inc(s_masks.sem, 1)
            dve.wait_ge(s_consts.sem, 1)
            dve.wait_ge(s_mask_add.sem, 1)
            dve.wait_ge(s_masks.sem, 1)

            def layer_norm_moments(batch, src, bn, mv, bn_done, mv_done):
                for t in range(T):
                    last = dve.bn_stats(bn[:, t, :], src[:, t, :])
                last.then_inc(bn_done.sem, 1)
                reached(dve, bn_done, batch)
                step_over(dve, dve_steps)
                for t in range(T):
                    last = dve.bn_aggr(mv[:, t, :], bn[:, t, :])
                last.then_inc(mv_done.sem, 1)

            def layer_norm_scale(dst, src, mv, inv_std, done):
                for t in range(T):
                    last = dve.tensor_scalar(dst[:, t, :], src[:, t, :], mv[:, t, 0:1], inv_std[:, t:t + 1],
                                             ALU.subtract, ALU.mult)
                last.then_inc(done.sem, 1)

            def heads_out(batch, group):
                heads = work_bank[:, :].rearrange("p (t h c) -> p t h c", t=T, h=HG)
                reached(dve, y_turned, batch, group + 1)
                dve.reciprocal(inv_den[:, :, :], heads[:, :, :, DH]).then_inc(den_ready.sem, 1)
                reached(dve, den_ready, batch, group + 1)
                reached(dve, yT_filled, batch - 1)
                dst = y_sb[:, :, group * HG * DH:(group + 1) * HG * DH]
                dve.tensor_tensor(dst.rearrange("p t (h c) -> p t h c", h=HG), heads[:, :, :, 0:DH],
                                  inv_den[:, :, :].unsqueeze(3).broadcast_to([P, T, HG, DH]),
                                  ALU.mult).then_inc(y_ready.sem, 1)

            def body(i, ahead, att, prev, old):
                for slot in range(SLOTS):
                    if att:
                        u = slot
                        reached(dve, scores_filled, i, u + 1)
                        reached(dve, probs_ready, i, u - 3)
                        step_over(dve, dve_steps)
                        dve.tensor_tensor_reduce(masked[:, u % 4, :], score_bank[u % 2][:, :],
                                                 mask_add[:, u % T, :], -SCALE, 3.0e38, ALU.add, ALU.min,
                                                 neg_max[:, u:u + 1]).then_inc(masked_ready.sem, 1)
                    batch, u = lagged(i, slot, TURN_LAG)
                    if u in VECTOR_UNITS and (att if slot >= TURN_LAG else prev):
                        reached(dve, turned, batch, u + 1)
                        reached(dve, pv_filled, batch - 1, u // (SLOTS // GROUPS) + 1)
                        h, t = divmod(u, T)
                        dve.tensor_copy(probs_t[:, h // HG, h % HG, :, t * P:(t + 1) * P],
                                        turn_bank[u % 2][:, :].rearrange("p (j q) -> p j q", j=T)
                                        ).then_inc(copied_vector.sem, 1)

                    if slot - 1 in COS_SLOTS and old:
                        m = COS_SLOTS.index(slot - 1)
                        reached(dve, cos_filled, i - 2, m + 1)
                        dve.scalar_tensor_tensor(adj_cos[:, m, :], adj_bank[0][:, :], 0.0, mask_t[:, m, :],
                                                 ALU.max, ALU.mult).then_inc(cos_ready.sem, 1)
                    if slot - 1 in RBF_SLOTS and old:
                        m = RBF_SLOTS.index(slot - 1)
                        reached(dve, rbf_filled, i - 2, m + 1)
                        if m == 0:
                            reached(dve, col_ready, i - 2)
                        if m >= 2:
                            reached(dve, rbf_exp_ready, i - 2, m - 1)
                        dve.tensor_tensor(rbf_arg[:, m % 2, :], adj_bank[1][:, :], col_term[:, :],
                                          ALU.add).then_inc(rbf_arg_ready.sem, 1)
                    if slot - 2 in RBF_SLOTS and old:
                        m = RBF_SLOTS.index(slot - 2)
                        reached(dve, rbf_exp_ready, i - 2, m + 1)
                        dve.scalar_tensor_tensor(adj_rbf[:, m, :], rbf_exp[:, m % 2, :], 1.0, mask_t[:, m, :],
                                                 ALU.min, ALU.mult).then_inc(rbf_ready.sem, 1)
                    if slot - 1 in MIX_SLOTS and old:
                        n = MIX_SLOTS.index(slot - 1)
                        src = adj_bank[n % 2]
                        reached(dve, mix_filled, i - 2, n + 1)
                        dve.tensor_tensor(degree[:, :], src[:, D:D + 258:257], degree_floor[:, :],
                                          ALU.max).then_inc(degree_ready.sem, 1)
                        reached(dve, degree_ready, i - 2, n + 1)
                        dve.reciprocal(inv_degree[:, :], degree[:, :]).then_inc(inv_degree_ready.sem, 1)
                        reached(dve, inv_degree_ready, i - 2, n + 1)
                        if n == 0:
                            reached(dve, x1_kept_ready, i - 2)
                            reached(dve, out_stored, i - 3)
                        dve.scalar_tensor_tensor(half_sum[:, :], src[:, 256:256 + D], inv_degree[:, 1:2],
                                                 x1_kept[:, n, :], ALU.mult,
                                                 ALU.add).then_inc(half_ready.sem, 1)
                        reached(dve, half_ready, i - 2, n + 1)
                        dve.scalar_tensor_tensor(out_sb[:, n, :], src[:, 0:D], inv_degree[:, 0:1],
                                                 half_sum[:, :], ALU.mult, ALU.add).then_inc(out_ready.sem, 1)

                    if slot == 6 and ahead:
                        reached(dve, x_loaded, i + 1)
                        layer_norm_moments(i + 1, x_sb, bn_sb, moments, ln_bn, ln_moments)
                    if slot == 8 and ahead:
                        reached(dve, ln_rstd, i + 1)
                        reached(dve, hT_filled, i)
                        layer_norm_scale(x_norm, x_sb, moments, rstd, ln_done)
                    if slot == 9 and att:
                        reached(dve, v_filled, i)
                        reached(dve, pv_filled, i - 1)
                        dve.tensor_tensor(v_cols[:, :, :, 0:DH],
                                          work_bank[:, :].rearrange("p (t h c) -> p t h c", t=T, h=H),
                                          bias_v[:, :].rearrange("p (h c) -> p h c", h=H).unsqueeze(1)
                                          .broadcast_to([P, T, H, DH]), ALU.add).then_inc(v_ready.sem, 1)
                    if slot == 10 and prev:
                        heads_out(i - 1, 1)
                    if slot in (13, 15) and ahead:
                        which = (slot - 13) // 2
                        reached(dve, qk_filled, i + 1, which + 1)
                        reached(dve, hi_ready, i + 1, which + 1)
                        reached(dve, lo_ready, i, which + 1)
                        dve.scalar_tensor_tensor(resid[:, which, :], work_bank[:, :],
                                                 (bias_q, bias_k)[which][:, 0:1], split[:, which, 0, :],
                                                 ALU.add, ALU.subtract).then_inc(rest_ready.sem, 1)
                    if slot == 14 and prev:
                        reached(dve, attn_filled, i - 1)
                        reached(dve, x_resid_ready, i - 1)
                        reached(dve, x1_kept_ready, i - 2)
                        dve.tensor_tensor(x1[:, :, :], work_bank[:, :].rearrange("p (t d) -> p t d", t=T),
                                          x_resid[:, :, :], ALU.add).then_inc(x1_ready.sem, 1)
                    if slot == 16 and prev:
                        reached(dve, x1_ready, i - 1)
                        layer_norm_moments(i - 1, x1, bn2_sb, moments2, ln2_bn, ln2_moments)
                    if slot == 18 and prev:
                        reached(dve, ln2_rstd, i - 1)
                        reached(dve, h2T_filled, i - 2)
                        layer_norm_scale(x1_norm, x1, moments2, rstd2, ln2_done)
                    if slot == 25 and prev:
                        reached(dve, z_squared, i - 1)
                        reached(dve, rbf_bias_ready, i - 2)
                        dve.tensor_reduce(square_sum[:, :, :],
                                          z_square[:, :, :].rearrange("p t (a d) -> p t a d", a=2), AX_X,
                                          ALU.add).then_inc(sums_ready.sem, 1)
                    if slot == 30 and att:
                        heads_out(i, 0)

            iterations(dve, body)

        @block.scalar
        def _(act):
            act.wait_ge(s_loaded.sem, 11 * 16)
            act.wait_ge(s_masks.sem, 1)
            act.wait_ge(s_consts.sem, 1)

            def body(i, ahead, att, prev, old):
                for slot in range(SLOTS):
                    if att:
                        u = slot
                        reached(act, masked_ready, i, u + 1)
                        reached(act, turned, i, u - 3)
                        act.activation(probs[:, u % 4, :], masked[:, u % 4, :], ACT.Exp,
                                       bias=neg_max[:, u:u + 1], scale=-1.0).then_inc(probs_ready.sem, 1)
                    batch, u = lagged(i, slot, TURN_LAG)
                    if u not in VECTOR_UNITS and (att if slot >= TURN_LAG else prev):
                        reached(act, turned, batch, u + 1)
                        reached(act, pv_filled, batch - 1, u // (SLOTS // GROUPS) + 1)
                        h, t = divmod(u, T)
                        act.copy(probs_t[:, h // HG, h % HG, :, t * P:(t + 1) * P],
                                 turn_bank[u % 2][:, :].rearrange("p (j q) -> p j q", j=T)
                                 ).then_inc(copied_scalar.sem, 1)

                    if slot - 1 in RBF_SLOTS and old:
                        m = RBF_SLOTS.index(slot - 1)
                        reached(act, rbf_arg_ready, i - 2, m + 1)
                        if m == 0:
                            reached(act, rbf_bias_ready, i - 2)
                        if m >= 2:
                            reached(act, rbf_ready, i - 2, m - 1)
                        act.activation(rbf_exp[:, m % 2, :], rbf_arg[:, m % 2, :], ACT.Exp,
                                       bias=rbf_bias[:, m:m + 1]).then_inc(rbf_exp_ready.sem, 1)
                    if slot == 8 and prev:
                        reached(act, pv_filled, i - 1, 2)
                        reached(act, y_turned, i - 1, 1)
                        act.copy(pv_sb[:, :], pv_bank[:, :]).then_inc(pv_copied.sem, 1)
                    if slot == 11 and ahead:
                        reached(act, hT_filled, i + 1)
                        act.activation(hT[:, :], work_bank[:, :], ACT.Relu).then_inc(hT_ready.sem, 1)
                    if slot == 12 and prev:
                        reached(act, yT_filled, i - 1)
                        act.copy(yT[:, :], work_bank[:, :]).then_inc(yT_ready.sem, 1)
                    if slot in (13, 15) and ahead:
                        which = (slot - 13) // 2
                        reached(act, qk_filled, i + 1, which + 1)
                        reached(act, split_stored, i, which + 1)
                        act.activation(split[:, which, 0, :], work_bank[:, :], ACT.Identity,
                                       bias=(bias_q, bias_k)[which][:, 0:1]).then_inc(hi_ready.sem, 1)
                    if slot == 20 and prev:
                        reached(act, h2T_filled, i - 1)
                        act.activation(h2T[:, :], work_bank[:, :], ACT.Relu).then_inc(h2T_ready.sem, 1)
                    if slot - 1 in Z_SLOTS and prev:
                        t = Z_SLOTS.index(slot - 1)
                        reached(act, z_filled, i - 1, t + 1)
                        act.copy(z[:, t, 0:3 * D], work_bank[:, 0:3 * D]).then_inc(z_ready.sem, 1)
                    if slot == 27 and prev:
                        reached(act, zgT_filled, i - 1)
                        act.copy(zgT[:, :], work_bank[:, :]).then_inc(zgT_ready.sem, 1)
                        act.activation(zgT_square[:, :], work_bank[:, :], ACT.Square
                                       ).then_inc(zgT_squared.sem, 1)
                    if slot == 28 and att:
                        reached(act, pv_filled, i, 1)
                        reached(act, y_turned, i - 1, 2)
                        act.copy(pv_sb[:, :], pv_bank[:, :]).then_inc(pv_copied.sem, 1)
                    if slot == 29 and prev:
                        reached(act, col_filled, i - 1)
                        reached(act, rbf_arg_ready, i - 2)
                        act.copy(col_term[:, :], work_bank[:, :]).then_inc(col_ready.sem, 1)
                    if slot == 31 and prev:
                        reached(act, zlT_filled, i - 1)
                        act.copy(zlT[:, :], work_bank[:, :]).then_inc(zlT_ready.sem, 1)

            iterations(act, body)


_INS = ["x", "adj", "L0_gnn_W_qkv", "L0_gnn_b_qkv", "L0_gnn_W_out", "L0_gnn_b_out",
        "L1_gnn_Wl", "L1_gnn_Wg", "L1_gnn_Wv", "L1_gnn_Wo"]
_OUTS = [((16, 512, 128), "float32")]


def kernel(**inputs):
    import numpy as _np
    import concourse.bacc as _bacc
    from concourse import mybir as _mybir
    from concourse.bass_utils import run_bass_kernel_spmd as _run

    nc = _bacc.Bacc("TRN2", target_bir_lowering=False, num_devices=1)
    arrays, args = {}, []
    for name in _INS:
        a = _np.ascontiguousarray(inputs[name])
        arrays[f"in_{name}_dram"] = a
        args.append(nc.dram_tensor(f"in_{name}_dram", a.shape, _mybir.dt.from_np(a.dtype), kind="ExternalInput").ap())
    for i, (shape, dtype) in enumerate(_OUTS):
        dt = _mybir.dt.from_np(_np.dtype(dtype))
        args.append(nc.dram_tensor(f"out_{i}_dram", shape, dt, kind="ExternalOutput").ap())
    graph_blocks(nc, *args)
    r = _run(nc, [arrays], core_ids=[0])
    got = tuple(r.results[0][f"out_{i}_dram"] for i in range(len(_OUTS)))
    return got[0]
```

```python
from contextlib import ExitStack

import concourse.bass as bass
from concourse import mybir

F32 = mybir.dt.float32
BF16 = mybir.dt.bfloat16
ALU = mybir.AluOpType
ACT = mybir.ActivationFunctionType
AX_X = mybir.AxisListType.X

P = 128
LN_EPS = 1e-5
KERNEL_EPS = 1e-8
W_LOCAL, W_GLOBAL = 0.9, 0.1
BIG = 2.0 ** 100
LEAST_SQUARE = KERNEL_EPS * KERNEL_EPS

Q_PARTS = (0, 0, 0, 1, 1, 2)
K_PARTS = (0, 1, 2, 0, 1, 0)

TURN_LAG = 3
VECTOR_UNITS = (3, 9, 21, 27)
AT = {
    "ln_moments": 0, "ln_rstd": 1, "ln_scale": 2, "hT": 3, "q": 6, "k": 9, "v": 17, "v_move": 13,
    "rbf": (1, 3, 10, 13), "rbf_exp": (2, 4, 11, 14), "rbf_mask": (3, 5, 12, 15), "cos": (2, 9, 12, 14),
    "pv1": (4, 5, 7, 8), "pv1_copy": 8, "y1": 11, "yT": 12, "attn": 14, "mix_cos": (15, 17, 19, 21),
    "mix_rbf": (16, 18, 20, 22), "ln2_moments": 15, "ln2_rstd": 19, "ln2_scale": 19, "h2T": 20,
    "z": (22, 23, 24, 25), "z_square": 25, "z_sums": 28, "z_norms": 28, "zgT": 27, "col": 30, "zlT": 31,
    "pv0": (23, 24, 25, 26), "pv0_copy": 26, "y0": 29, "resid_move": 17, "x_biased": 18, "x1_keep": 23,
}


class Signal:

    def __init__(self, sem, per, step):
        self.sem, self.per, self.step = sem, per, step


def reached(engine, signal, batch, nth=None):
    count = (batch * signal.per + (signal.per if nth is None else nth)) * signal.step
    if isinstance(count, int) and count <= 0:
        return
    engine.wait_ge(signal.sem, count)


def graph_blocks(nc, x, adj, w_qkv, b_qkv, w_out, b_out, w_l, w_g, w_v, w_o, out):
    B, N, D = x.shape
    H = 8
    DH = D // H
    T = N // P
    GROUPS = 2
    HG = H // GROUPS
    SLOTS = H * T
    ROWS = len(Q_PARTS) * DH
    HALF = H // 2
    SCALE = float(DH) ** -0.5
    ZC = 3 * D + 2
    assert D == P and T == 4 and HG * 32 == P

    copied_by_vector = [u for u in range(SLOTS) if u in VECTOR_UNITS]
    copied_by_scalar = [u for u in range(SLOTS) if u not in VECTOR_UNITS]

    with ExitStack() as ctx:
        def sb(name, shape, dt=F32):
            return ctx.enter_context(nc.sbuf_tensor(name, shape, dt))

        def bank(name):
            return ctx.enter_context(nc.psum_tensor(name, [P, 512], F32))

        def signal(name, per=1, step=1):
            return Signal(ctx.enter_context(nc.semaphore(name)), per, step)

        wqkv_sb = sb("wqkv_sb", [P, 3 * D])
        wz_sb = sb("wz_sb", [P, 3 * D])
        wout_sb = sb("wout_sb", [P, D])
        wv_sb = sb("wv_sb", [P, D])
        wo_sb = sb("wo_sb", [P, D])
        wvT_sb = sb("wvT_sb", [P, D])
        bias_q = sb("bias_q", [P, 1])
        bias_k = sb("bias_k", [P, 1])
        bias_v = sb("bias_v", [P, D])
        bias_out = sb("bias_out", [P, D])
        ident = sb("ident", [P, P])
        neg_half = sb("neg_half", [P, P])
        minus_half = sb("minus_half", [P, T])
        degree_floor = sb("degree_floor", [P, 2])
        adj_sb = sb("adj_sb", [P, T, N], adj.dtype)
        mask_add = sb("mask_add", [P, T, N], BF16)
        mask_t = sb("mask_t", [P, T, N], BF16)

        x_sb = sb("x_sb", [P, T, D])
        bn_sb = sb("bn_sb", [P, T, 6])
        moments = sb("moments", [P, T, 2])
        var_eps = sb("var_eps", [P, T])
        rstd = sb("rstd", [P, T])
        x_norm = sb("x_norm", [P, T, D])
        x_biased = sb("x_biased", [P, T, D])
        x_resid = sb("x_resid", [P, T, D])
        hT = sb("hT", [P, N])
        split = sb("split", [P, 2, 3, N], BF16)
        resid = sb("resid", [P, 2, N])
        qk_rows = sb("qk_rows", [ROWS, 2, H, N], BF16)
        v_stage = sb("v_stage", [P, T, D])
        v_cols = sb("v_cols", [P, T, H, 32])
        masked = sb("masked", [P, 4, N])
        neg_max = sb("neg_max", [P, SLOTS])
        probs = sb("probs", [P, 4, N])
        probs_t = sb("probs_t", [P, GROUPS, HG, T, N])
        pv_sb = sb("pv_sb", [P, N])
        inv_den = sb("inv_den", [P, T, HG])
        y_sb = sb("y_sb", [P, T, D])
        yT = sb("yT", [P, N])

        x1 = sb("x1", [P, T, D])
        x1_kept = sb("x1_kept", [P, T, D])
        bn2_sb = sb("bn2_sb", [P, T, 6])
        moments2 = sb("moments2", [P, T, 2])
        var_eps2 = sb("var_eps2", [P, T])
        rstd2 = sb("rstd2", [P, T])
        x1_norm = sb("x1_norm", [P, T, D])
        h2T = sb("h2T", [P, N])
        z = sb("z", [P, T, ZC])
        z_square = sb("z_square", [P, T, 2 * D])
        square_sum = sb("square_sum", [P, T, 2])
        norm_floor = sb("norm_floor", [P, T])
        inv_norm = sb("inv_norm", [P, T])
        rbf_bias = sb("rbf_bias", [P, T])
        zl_unit = sb("zl_unit", [P, T, D])
        zlT = sb("zlT", [P, N])
        zgT = sb("zgT", [P, N])
        zgT_square = sb("zgT_square", [P, N])
        col_term = sb("col_term", [P, N])
        rbf_arg = sb("rbf_arg", [P, 2, N])
        rbf_exp = sb("rbf_exp", [P, 2, N])
        adj_cos = sb("adj_cos", [P, T, N])
        adj_rbf = sb("adj_rbf", [P, T, N])
        degree = sb("degree", [P, 2])
        inv_degree = sb("inv_degree", [P, 2])
        half_sum = sb("half_sum", [P, D])
        out_sb = sb("out_sb", [P, T, D])

        split_dram = nc.dram_tensor("split_dram", (2, 3, P, N), BF16, kind="Internal").ap()

        score_bank = [bank("score0"), bank("score1")]
        turn_bank = [bank("turn0"), bank("turn1")]
        pv_bank = bank("pv")
        work_bank = bank("work")
        adj_bank = [bank("adj0"), bank("adj1")]

        s_loaded = signal("setup_loaded", 12, 16)
        s_consts = signal("setup_consts")
        s_ident = signal("setup_ident", 2)
        s_zeroed = signal("setup_zeroed")
        s_adj_cast = signal("setup_adj_cast")
        s_adj_open = signal("setup_adj_open")
        s_adj_turned = signal("setup_adj_turned", T)
        s_mask_add = signal("setup_mask_add")
        s_masks = signal("setup_masks")
        s_wv_turned = signal("setup_wv_turned")
        s_wv_copied = signal("setup_wv_copied")
        s_wvo = signal("setup_wvo")
        s_wvo_copied = signal("setup_wvo_copied")

        dve_steps = signal("dve_steps")
        pool_steps = signal("pool_steps")

        x_loaded = signal("x_loaded", 1, 16)
        ln_bn = signal("ln_bn")
        ln_moments = signal("ln_moments")
        ln_var = signal("ln_var")
        ln_rstd = signal("ln_rstd")
        ln_done = signal("ln_done")
        x_biased_ready = signal("x_biased_ready")
        x_resid_ready = signal("x_resid_ready")
        hT_filled = signal("hT_filled")
        hT_ready = signal("hT_ready")
        qk_filled = signal("qk_filled", 2)
        hi_ready = signal("hi_ready", 2)
        rest_ready = signal("rest_ready", 2)
        mid_ready = signal("mid_ready", 2)
        lo_ready = signal("lo_ready", 2)
        split_stored = signal("split_stored", 2, 16)
        rows_loaded = [signal(f"rows_loaded{h}", 2 * len(Q_PARTS), 16) for h in range(2)]

        v_filled = signal("v_filled")
        v_staged = signal("v_staged")
        v_ready = signal("v_ready")
        scores_filled = signal("scores_filled", SLOTS)
        masked_ready = signal("masked_ready", SLOTS)
        probs_ready = signal("probs_ready", SLOTS)
        turned = signal("turned", SLOTS)
        copied_vector = signal("copied_vector", len(copied_by_vector))
        copied_scalar = signal("copied_scalar", len(copied_by_scalar))
        pv_filled = signal("pv_filled", GROUPS)
        pv_copied = signal("pv_copied", GROUPS)
        y_turned = signal("y_turned", GROUPS)
        den_ready = signal("den_ready", GROUPS)
        y_ready = signal("y_ready", GROUPS)
        yT_filled = signal("yT_filled")
        yT_ready = signal("yT_ready")
        attn_filled = signal("attn_filled")
        x1_ready = signal("x1_ready")
        x1_kept_ready = signal("x1_kept_ready")

        ln2_bn = signal("ln2_bn")
        ln2_moments = signal("ln2_moments")
        ln2_var = signal("ln2_var")
        ln2_rstd = signal("ln2_rstd")
        ln2_done = signal("ln2_done")
        h2T_filled = signal("h2T_filled")
        h2T_ready = signal("h2T_ready")
        z_filled = signal("z_filled", T)
        z_ready = signal("z_ready", T)
        z_squared = signal("z_squared")
        sums_ready = signal("sums_ready")
        floor_ready = signal("floor_ready")
        rbf_bias_ready = signal("rbf_bias_ready")
        inv_norm_ready = signal("inv_norm_ready")
        unit_ready = signal("unit_ready")
        zgT_filled = signal("zgT_filled")
        zgT_ready = signal("zgT_ready")
        zgT_squared = signal("zgT_squared")
        col_filled = signal("col_filled")
        col_ready = signal("col_ready")
        zlT_filled = signal("zlT_filled")
        zlT_ready = signal("zlT_ready")
        cos_filled = signal("cos_filled", T)
        cos_ready = signal("cos_ready", T)
        rbf_filled = signal("rbf_filled", T)
        rbf_arg_ready = signal("rbf_arg_ready", T)
        rbf_exp_ready = signal("rbf_exp_ready", T)
        rbf_ready = signal("rbf_ready", T)
        mix_filled = signal("mix_filled", T)
        degree_ready = signal("degree_ready", T)
        inv_degree_ready = signal("inv_degree_ready", T)
        half_ready = signal("half_ready", T)
        out_ready = signal("out_ready", T)
        out_stored = signal("out_stored", 1, 16)

        def step_over(engine, counter):
            engine.sem_inc(counter.sem, 1)

        def lagged(i, slot, lag):
            return (i, slot - lag) if slot >= lag else (i - 1, slot - lag + SLOTS)

        def copies_reached(engine, batch, last):
            by_vector = sum(u <= last for u in copied_by_vector)
            by_scalar = sum(u <= last for u in copied_by_scalar)
            if by_vector:
                reached(engine, copied_vector, batch, by_vector)
            if by_scalar:
                reached(engine, copied_scalar, batch, by_scalar)

        def iterations(engine, body):
            for i in (-1, 0, 1, 2):
                body(i, i + 1 < B, 0 <= i, 1 <= i, 2 <= i)
            with engine.Fori(3, B - 2) as i:
                body(i, True, True, True, True)
            for i in (B - 2, B - 1, B, B + 1):
                body(i, i + 1 < B, i < B, i - 1 < B, True)

        WORK_USES = sorted(
            [("hT", hT_ready, 1, 1), ("q", rest_ready, 1, 1), ("k", rest_ready, 2, 1), ("v", v_staged, 1, 1),
             ("y1", y_ready, 2, -1), ("yT", yT_ready, 1, -1), ("attn", x1_ready, 1, -1),
             ("h2T", h2T_ready, 1, -1), ("zgT", zgT_squared, 1, -1), ("col", col_ready, 1, -1),
             ("y0", y_ready, 1, 0), ("zlT", zlT_ready, 1, -1)], key=lambda use: AT[use[0]])

        def work_bank_free(engine, i, use):
            at = [name for name, _, _, _ in WORK_USES].index(use)
            for back in range(1, len(WORK_USES) + 1):
                _, sig, nth, offset = WORK_USES[(at - back) % len(WORK_USES)]
                batch = i + offset - (1 if back > at else 0)
                if isinstance(batch, int) and not 0 <= batch < B:
                    continue
                reached(engine, sig, batch, nth)
                return

        block = ctx.enter_context(nc.Block())

        @block.sync
        def _(sp):
            for dst, src in (
                (adj_sb[:, :, :], adj.rearrange("(t p) k -> p t k", p=P)),
                (wqkv_sb[:, :], w_qkv),
                (wout_sb[:, :], w_out),
                (wz_sb[:, 0:D], w_l),
                (wz_sb[:, D:2 * D], w_g),
                (wv_sb[:, :], w_v),
                (wo_sb[:, :], w_o),
                (bias_q[:, :], b_qkv[0:D].rearrange("(p o) -> p o", o=1)),
                (bias_k[:, :], b_qkv[D:2 * D].rearrange("(p o) -> p o", o=1)),
                (bias_v[:, :], b_qkv[2 * D:3 * D].partition_broadcast(P)),
                (bias_out[:, :], b_out.partition_broadcast(P)),
            ):
                sp.dma_start(dst, src).then_inc(s_loaded.sem, 16)

            def load_x(batch):
                sp.dma_start(x_sb[:, :, :], x[batch].rearrange("(t p) d -> p t d", p=P)).then_inc(x_loaded.sem, 16)

            def load_rows(batch, half):
                h0 = half * HALF
                for which, parts in enumerate((Q_PARTS, K_PARTS)):
                    for block_row, part in enumerate(parts):
                        src = split_dram[which, part, h0 * DH:(h0 + HALF) * DH, :]
                        sp.dma_start(qk_rows[block_row * DH:(block_row + 1) * DH, which, h0:h0 + HALF, :],
                                     src.rearrange("(h f) n -> f h n", f=DH)).then_inc(rows_loaded[half].sem, 16)

            load_x(0)

            def body(i, ahead, att, prev, old):
                if ahead:
                    reached(sp, rows_loaded[0], i)
                    reached(sp, rows_loaded[1], i)
                    for which in range(2):
                        reached(sp, lo_ready, i + 1, which + 1)
                        reached(sp, hi_ready, i + 1, which + 1)
                        sp.dma_start(split_dram[which].rearrange("c f n -> f c n"),
                                     split[:, which, :, :]).then_inc(split_stored.sem, 16)
                    reached(sp, split_stored, i + 1)
                    reached(sp, scores_filled, i, SLOTS // 2)
                    load_rows(i + 1, 0)
                if old:
                    reached(sp, out_ready, i - 2)
                    sp.dma_start(out[i - 2].rearrange("(t p) d -> p t d", p=P),
                                 out_sb[:, :, :]).then_inc(out_stored.sem, 16)
                if ahead:
                    if not (isinstance(i, int) and i + 2 >= B):
                        reached(sp, ln_done, i + 1)
                        reached(sp, x_biased_ready, i + 1)
                        load_x(i + 2)
                    reached(sp, scores_filled, i, SLOTS)
                    load_rows(i + 1, 1)

            iterations(sp, body)
            reached(sp, out_stored, B - 1)
            reached(sp, split_stored, B - 1)

        @block.gpsimd
        def _(pool):
            pool.memset(ident[:, :], 0.0)
            pool.memset(neg_half[:, :], -0.5)
            pool.memset(minus_half[:, :], -0.5)
            pool.memset(degree_floor[:, 0:1], KERNEL_EPS / W_LOCAL)
            pool.memset(degree_floor[:, 1:2], KERNEL_EPS / W_GLOBAL)
            pool.memset(z[:, :, 3 * D:3 * D + 1], 1.0 / W_LOCAL)
            pool.memset(z[:, :, 3 * D + 1:ZC], 1.0 / W_GLOBAL)
            pool.memset(v_cols[:, :, :, DH + 1:32], 0.0)
            pool.memset(v_cols[:, :, :, DH:DH + 1], 1.0).then_inc(s_consts.sem, 1)
            pool.wait_ge(s_consts.sem, 1)
            pool.affine_select(out=ident[:, :], in_=ident[:, :], compare_op=ALU.not_equal, fill=1.0, base=0,
                               pattern=[[-1, P]], channel_multiplier=1).then_inc(s_ident.sem, 1)
            pool.wait_ge(s_adj_cast.sem, 1)
            pool.affine_select(out=probs[:, :, :], in_=probs[:, :, :], compare_op=ALU.not_equal, fill=0.0,
                               base=0, pattern=[[P, T], [-1, N]],
                               channel_multiplier=1).then_inc(s_adj_open.sem, 1)
            pool.wait_ge(s_loaded.sem, 11 * 16)

            def body(i, ahead, att, prev, old):
                for slot in range(SLOTS):
                    if slot == AT["ln_rstd"] and ahead:
                        reached(pool, ln_moments, i + 1)
                        reached(pool, ln_done, i)
                        step_over(pool, pool_steps)
                        pool.tensor_scalar(var_eps[:, :], moments[:, :, 1], LN_EPS, None,
                                           ALU.add).then_inc(ln_var.sem, 1)
                        reached(pool, ln_var, i + 1)
                        pool.tensor_tensor(rstd[:, :], var_eps[:, :], minus_half[:, :],
                                           ALU.pow).then_inc(ln_rstd.sem, 1)
                    if slot in (AT["q"], AT["k"]) and ahead:
                        which = (AT["q"], AT["k"]).index(slot)
                        reached(pool, split_stored, i, which + 1)
                        reached(pool, rest_ready, i + 1, which + 1)
                        step_over(pool, pool_steps)
                        pool.tensor_copy(split[:, which, 1, :], resid[:, which, :]).then_inc(mid_ready.sem, 1)
                        reached(pool, mid_ready, i + 1, which + 1)
                        pool.tensor_tensor(split[:, which, 2, :], resid[:, which, :], split[:, which, 1, :],
                                           ALU.subtract).then_inc(lo_ready.sem, 1)
                    if slot == AT["v_move"] and att:
                        reached(pool, v_staged, i)
                        reached(pool, pv_filled, i - 1)
                        step_over(pool, pool_steps)
                        pool.tensor_copy(v_cols[:, :, :, 0:DH], v_stage[:, :, :].rearrange(
                            "p t (h c) -> p t h c", h=H)).then_inc(v_ready.sem, 1)
                    if slot == AT["ln2_rstd"] and prev:
                        reached(pool, ln2_moments, i - 1)
                        reached(pool, ln2_done, i - 2)
                        step_over(pool, pool_steps)
                        pool.tensor_scalar(var_eps2[:, :], moments2[:, :, 1], LN_EPS, None,
                                           ALU.add).then_inc(ln2_var.sem, 1)
                        reached(pool, ln2_var, i - 1)
                        pool.tensor_tensor(rstd2[:, :], var_eps2[:, :], minus_half[:, :],
                                           ALU.pow).then_inc(ln2_rstd.sem, 1)
                    if slot == AT["resid_move"] and att:
                        reached(pool, x1_ready, i - 1)
                        reached(pool, x_biased_ready, i)
                        step_over(pool, pool_steps)
                        pool.tensor_copy(x_resid[:, :, :], x_biased[:, :, :]).then_inc(x_resid_ready.sem, 1)
                    if slot == AT["x_biased"] and ahead:
                        reached(pool, x_loaded, i + 1)
                        reached(pool, x_resid_ready, i)
                        pool.tensor_tensor(x_biased[:, :, :], x_sb[:, :, :],
                                           bias_out[:, :].unsqueeze(1).broadcast_to([P, T, D]),
                                           ALU.add).then_inc(x_biased_ready.sem, 1)
                    if slot == AT["x1_keep"] and prev:
                        reached(pool, x1_ready, i - 1)
                        reached(pool, out_ready, i - 2)
                        step_over(pool, pool_steps)
                        pool.tensor_copy(x1_kept[:, :, :], x1[:, :, :]).then_inc(x1_kept_ready.sem, 1)
                    if slot == AT["z_square"] and prev:
                        reached(pool, z_ready, i - 1)
                        reached(pool, sums_ready, i - 2)
                        pool.tensor_tensor(z_square[:, :, :], z[:, :, 0:2 * D], z[:, :, 0:2 * D],
                                           ALU.mult).then_inc(z_squared.sem, 1)
                    if slot == AT["z_norms"] and prev:
                        reached(pool, sums_ready, i - 1)
                        step_over(pool, pool_steps)
                        pool.tensor_scalar(norm_floor[:, :], square_sum[:, :, 0], LEAST_SQUARE, None,
                                           ALU.max).then_inc(floor_ready.sem, 1)
                        reached(pool, rbf_exp_ready, i - 2)
                        step_over(pool, pool_steps)
                        pool.tensor_scalar(rbf_bias[:, :], square_sum[:, :, 1], -0.5, None,
                                           ALU.mult).then_inc(rbf_bias_ready.sem, 1)
                        reached(pool, floor_ready, i - 1)
                        pool.tensor_tensor(inv_norm[:, :], norm_floor[:, :], minus_half[:, :],
                                           ALU.pow).then_inc(inv_norm_ready.sem, 1)
                        reached(pool, inv_norm_ready, i - 1)
                        reached(pool, zlT_filled, i - 2)
                        pool.tensor_tensor(zl_unit[:, :, :], z[:, :, 0:D],
                                           inv_norm[:, :].unsqueeze(2).broadcast_to([P, T, D]),
                                           ALU.mult).then_inc(unit_ready.sem, 1)

            iterations(pool, body)

        @block.tensor
        def _(pe):
            pe.wait_ge(s_ident.sem, 1)
            pe.wait_ge(s_loaded.sem, 11 * 16)
            pe.transpose(adj_bank[0][:, 0:D], wv_sb[:, :], ident[:, :]).then_inc(s_wv_turned.sem, 1)
            pe.wait_ge(s_wv_copied.sem, 1)
            pe.matmul(adj_bank[1][:, 0:D], wvT_sb[:, :], wo_sb[:, :], start=True,
                      stop=True).then_inc(s_wvo.sem, 1)
            pe.wait_ge(s_adj_open.sem, 1)
            for m, dst in enumerate(score_bank + turn_bank):
                for t in range(T):
                    last = pe.transpose(dst[:, t * P:(t + 1) * P], probs[:, t, m * P:(m + 1) * P], ident[:, :])
                last.then_inc(s_adj_turned.sem, 1)
            pe.wait_ge(s_masks.sem, 1)
            pe.wait_ge(s_wvo_copied.sem, 1)

            def scores(batch, u):
                h, t = divmod(u, T)
                if u % (SLOTS // 2) == 0:
                    reached(pe, rows_loaded[u // (SLOTS // 2)], batch)
                reached(pe, masked_ready, batch, u - 1)
                pe.matmul(score_bank[u % 2][:, :], qk_rows[:, 0, h, t * P:(t + 1) * P], qk_rows[:, 1, h, :],
                          start=True, stop=True).then_inc(scores_filled.sem, 1)

            def turn(batch, u):
                reached(pe, probs_ready, batch, u + 1)
                if u >= 2:
                    copies_reached(pe, batch, u - 2)
                else:
                    copies_reached(pe, batch - 1, SLOTS + u - 2)
                for j in range(T):
                    last = pe.transpose(turn_bank[u % 2][:, j * P:(j + 1) * P],
                                        probs[:, u % 4, j * P:(j + 1) * P], ident[:, :])
                last.then_inc(turned.sem, 1)

            def attend(batch, group, j):
                if j == 0:
                    copies_reached(pe, batch, (group + 1) * SLOTS // GROUPS - 1)
                    reached(pe, v_ready, batch)
                    reached(pe, pv_copied, batch, group)
                for hl in range(HG):
                    last = pe.matmul(pv_bank[32 * hl:32 * (hl + 1), :], v_cols[:, j, group * HG + hl, :],
                                     probs_t[:, group, hl, j, :], start=(j == 0), stop=(j == T - 1),
                                     tile_position=(0, 32 * hl))
                if j == T - 1:
                    last.then_inc(pv_filled.sem, 1)

            def mix(n, at, adjacency):
                for m in range(T):
                    last = pe.matmul(adj_bank[n % 2][:, at:at + D + 2], adjacency[:, m, n * P:(n + 1) * P],
                                     z[:, m, 2 * D:ZC], start=(m == 0), stop=(m == T - 1))
                return last

            def turn_tiles(src, ready):
                for t in range(T):
                    last = pe.transpose(work_bank[:, t * P:(t + 1) * P], src(t), ident[:, :])
                last.then_inc(ready.sem, 1)

            def body(i, ahead, att, prev, old):
                for slot in range(SLOTS):
                    if att:
                        scores(i, slot)
                    batch, u = lagged(i, slot, TURN_LAG)
                    if (att if slot >= TURN_LAG else prev):
                        turn(batch, u)

                    if slot in AT["cos"] and old:
                        m = AT["cos"].index(slot)
                        if m == 0:
                            reached(pe, zlT_ready, i - 2)
                            reached(pe, z_ready, i - 2, T - 1)
                        else:
                            reached(pe, cos_ready, i - 2, m)
                        pe.matmul(adj_bank[0][:, :], zlT[:, m * P:(m + 1) * P], zlT[:, :], start=True,
                                  stop=True).then_inc(cos_filled.sem, 1)
                    if slot in AT["rbf"] and old:
                        m = AT["rbf"].index(slot)
                        if m == 0:
                            reached(pe, zgT_ready, i - 2)
                            reached(pe, z_ready, i - 2, T)
                        else:
                            reached(pe, rbf_arg_ready, i - 2, m)
                        pe.matmul(adj_bank[1][:, :], zgT[:, m * P:(m + 1) * P], zgT[:, :], start=True,
                                  stop=True).then_inc(rbf_filled.sem, 1)
                    if slot in AT["mix_cos"] and old:
                        n = AT["mix_cos"].index(slot)
                        if n == 0:
                            reached(pe, cos_ready, i - 2)
                        elif n == 1:
                            reached(pe, rbf_arg_ready, i - 2)
                        else:
                            reached(pe, out_ready, i - 2, n - 1)
                        mix(n, 0, adj_cos)
                    if slot in AT["mix_rbf"] and old:
                        n = AT["mix_rbf"].index(slot)
                        if n == 0:
                            reached(pe, rbf_ready, i - 2)
                        mix(n, 256, adj_rbf).then_inc(mix_filled.sem, 1)

                    if slot in AT["pv1"] and prev:
                        attend(i - 1, 1, AT["pv1"].index(slot))
                    if slot in AT["pv0"] and att:
                        attend(i, 0, AT["pv0"].index(slot))

                    if slot == AT["hT"] and ahead:
                        reached(pe, ln_done, i + 1)
                        work_bank_free(pe, i, "hT")
                        turn_tiles(lambda t: x_norm[:, t, :], hT_filled)
                    if slot in (AT["q"], AT["k"]) and ahead:
                        which = (AT["q"], AT["k"]).index(slot)
                        reached(pe, hT_ready, i + 1)
                        work_bank_free(pe, i, "qk"[which])
                        pe.matmul(work_bank[:, :], wqkv_sb[:, which * D:(which + 1) * D], hT[:, :], start=True,
                                  stop=True).then_inc(qk_filled.sem, 1)
                    if slot == AT["v"] and ahead:
                        reached(pe, hT_ready, i + 1)
                        work_bank_free(pe, i, "v")
                        for t in range(T):
                            last = pe.matmul(work_bank[:, t * P:(t + 1) * P], hT[:, t * P:(t + 1) * P],
                                             wqkv_sb[:, 2 * D:3 * D], start=True, stop=True)
                        last.then_inc(v_filled.sem, 1)
                    if slot == AT["y1"] and prev:
                        reached(pe, pv_copied, i - 1, 2)
                        work_bank_free(pe, i, "y1")
                        turn_tiles(lambda t: pv_sb[:, t * P:(t + 1) * P], y_turned)
                    if slot == AT["yT"] and prev:
                        reached(pe, y_ready, i - 1, 2)
                        work_bank_free(pe, i, "yT")
                        turn_tiles(lambda t: y_sb[:, t, :], yT_filled)
                    if slot == AT["attn"] and prev:
                        reached(pe, yT_ready, i - 1)
                        work_bank_free(pe, i, "attn")
                        for t in range(T):
                            last = pe.matmul(work_bank[:, t * P:(t + 1) * P], yT[:, t * P:(t + 1) * P],
                                             wout_sb[:, :], start=True, stop=True)
                        last.then_inc(attn_filled.sem, 1)
                    if slot == AT["h2T"] and prev:
                        reached(pe, ln2_done, i - 1)
                        work_bank_free(pe, i, "h2T")
                        turn_tiles(lambda t: x1_norm[:, t, :], h2T_filled)
                    if slot in AT["z"] and prev:
                        t = AT["z"].index(slot)
                        reached(pe, h2T_ready, i - 1)
                        if t < 2:
                            reached(pe, out_ready, i - 2, t + 3)
                        else:
                            reached(pe, z_ready, i - 1, t - 1)
                        pe.matmul(adj_bank[t % 2][:, 0:3 * D], h2T[:, t * P:(t + 1) * P], wz_sb[:, :],
                                  start=True, stop=True).then_inc(z_filled.sem, 1)
                    if slot == AT["zgT"] and prev:
                        reached(pe, z_ready, i - 1)
                        work_bank_free(pe, i, "zgT")
                        turn_tiles(lambda t: z[:, t, D:2 * D], zgT_filled)
                    if slot == AT["col"] and prev:
                        reached(pe, zgT_squared, i - 1)
                        work_bank_free(pe, i, "col")
                        pe.matmul(work_bank[:, :], neg_half[:, :], zgT_square[:, :], start=True,
                                  stop=True).then_inc(col_filled.sem, 1)
                    if slot == AT["y0"] and att:
                        reached(pe, pv_copied, i, 1)
                        work_bank_free(pe, i, "y0")
                        turn_tiles(lambda t: pv_sb[:, t * P:(t + 1) * P], y_turned)
                    if slot == AT["zlT"] and prev:
                        reached(pe, unit_ready, i - 1)
                        work_bank_free(pe, i, "zlT")
                        turn_tiles(lambda t: zl_unit[:, t, :], zlT_filled)

            iterations(pe, body)

        @block.vector
        def _(dve):
            dve.wait_ge(s_loaded.sem, 11 * 16)
            dve.tensor_copy(probs[:, :, :], adj_sb[:, :, :]).then_inc(s_adj_cast.sem, 1)
            dve.tensor_scalar(mask_add[:, :, :], adj_sb[:, :, :], BIG, -BIG, ALU.mult,
                              ALU.add).then_inc(s_mask_add.sem, 1)
            dve.wait_ge(s_wv_turned.sem, 1)
            dve.tensor_copy(wvT_sb[:, :], adj_bank[0][:, 0:D]).then_inc(s_wv_copied.sem, 1)
            dve.wait_ge(s_wvo.sem, 1)
            dve.tensor_copy(wz_sb[:, 2 * D:3 * D], adj_bank[1][:, 0:D]).then_inc(s_wvo_copied.sem, 1)
            for m, src in enumerate(score_bank + turn_bank):
                dve.wait_ge(s_adj_turned.sem, m + 1)
                last = dve.tensor_copy(mask_t[:, m, :], src[:, :])
            last.then_inc(s_masks.sem, 1)
            dve.wait_ge(s_consts.sem, 1)
            dve.wait_ge(s_mask_add.sem, 1)
            dve.wait_ge(s_masks.sem, 1)

            def layer_norm_moments(batch, src, bn, mv, bn_done, mv_done):
                for t in range(T):
                    last = dve.bn_stats(bn[:, t, :], src[:, t, :])
                last.then_inc(bn_done.sem, 1)
                reached(dve, bn_done, batch)
                step_over(dve, dve_steps)
                for t in range(T):
                    last = dve.bn_aggr(mv[:, t, :], bn[:, t, :])
                last.then_inc(mv_done.sem, 1)

            def layer_norm_scale(dst, src, mv, inv_std, done):
                for t in range(T):
                    last = dve.tensor_scalar(dst[:, t, :], src[:, t, :], mv[:, t, 0:1], inv_std[:, t:t + 1],
                                             ALU.subtract, ALU.mult)
                last.then_inc(done.sem, 1)

            def heads_out(batch, group):
                heads = work_bank[:, :].rearrange("p (t h c) -> p t h c", t=T, h=HG)
                reached(dve, y_turned, batch, group + 1)
                dve.reciprocal(inv_den[:, :, :], heads[:, :, :, DH]).then_inc(den_ready.sem, 1)
                reached(dve, den_ready, batch, group + 1)
                reached(dve, yT_filled, batch - 1)
                dst = y_sb[:, :, group * HG * DH:(group + 1) * HG * DH]
                dve.tensor_tensor(dst.rearrange("p t (h c) -> p t h c", h=HG), heads[:, :, :, 0:DH],
                                  inv_den[:, :, :].unsqueeze(3).broadcast_to([P, T, HG, DH]),
                                  ALU.mult).then_inc(y_ready.sem, 1)

            def body(i, ahead, att, prev, old):
                for slot in range(SLOTS):
                    if att:
                        u = slot
                        reached(dve, scores_filled, i, u + 1)
                        reached(dve, probs_ready, i, u - 3)
                        step_over(dve, dve_steps)
                        dve.tensor_tensor_reduce(masked[:, u % 4, :], score_bank[u % 2][:, :],
                                                 mask_add[:, u % T, :], -SCALE, 3.0e38, ALU.add, ALU.min,
                                                 neg_max[:, u:u + 1]).then_inc(masked_ready.sem, 1)
                    batch, u = lagged(i, slot, TURN_LAG)
                    if u in VECTOR_UNITS and (att if slot >= TURN_LAG else prev):
                        reached(dve, turned, batch, u + 1)
                        reached(dve, pv_filled, batch - 1, u // (SLOTS // GROUPS) + 1)
                        h, t = divmod(u, T)
                        dve.tensor_copy(probs_t[:, h // HG, h % HG, :, t * P:(t + 1) * P],
                                        turn_bank[u % 2][:, :].rearrange("p (j q) -> p j q", j=T)
                                        ).then_inc(copied_vector.sem, 1)

                    if slot in AT["cos"] and old:
                        m = AT["cos"].index(slot)
                        reached(dve, cos_filled, i - 2, m + 1)
                        dve.scalar_tensor_tensor(adj_cos[:, m, :], adj_bank[0][:, :], 0.0, mask_t[:, m, :],
                                                 ALU.max, ALU.mult).then_inc(cos_ready.sem, 1)
                    if slot in AT["rbf"] and old:
                        m = AT["rbf"].index(slot)
                        reached(dve, rbf_filled, i - 2, m + 1)
                        if m == 0:
                            reached(dve, col_ready, i - 2)
                        if m >= 2:
                            reached(dve, rbf_exp_ready, i - 2, m - 1)
                        dve.tensor_tensor(rbf_arg[:, m % 2, :], adj_bank[1][:, :], col_term[:, :],
                                          ALU.add).then_inc(rbf_arg_ready.sem, 1)
                    if slot in AT["rbf_mask"] and old:
                        m = AT["rbf_mask"].index(slot)
                        reached(dve, rbf_exp_ready, i - 2, m + 1)
                        dve.scalar_tensor_tensor(adj_rbf[:, m, :], rbf_exp[:, m % 2, :], 1.0, mask_t[:, m, :],
                                                 ALU.min, ALU.mult).then_inc(rbf_ready.sem, 1)
                    if slot in AT["mix_rbf"] and old:
                        n = AT["mix_rbf"].index(slot)
                        src = adj_bank[n % 2]
                        reached(dve, mix_filled, i - 2, n + 1)
                        dve.tensor_tensor(degree[:, :], src[:, D:D + 258:257], degree_floor[:, :],
                                          ALU.max).then_inc(degree_ready.sem, 1)
                        reached(dve, degree_ready, i - 2, n + 1)
                        dve.reciprocal(inv_degree[:, :], degree[:, :]).then_inc(inv_degree_ready.sem, 1)
                        reached(dve, inv_degree_ready, i - 2, n + 1)
                        if n == 0:
                            reached(dve, x1_kept_ready, i - 2)
                            reached(dve, out_stored, i - 3)
                        dve.scalar_tensor_tensor(half_sum[:, :], src[:, 256:256 + D], inv_degree[:, 1:2],
                                                 x1_kept[:, n, :], ALU.mult,
                                                 ALU.add).then_inc(half_ready.sem, 1)
                        reached(dve, half_ready, i - 2, n + 1)
                        dve.scalar_tensor_tensor(out_sb[:, n, :], src[:, 0:D], inv_degree[:, 0:1],
                                                 half_sum[:, :], ALU.mult, ALU.add).then_inc(out_ready.sem, 1)

                    if slot == AT["ln_moments"] and ahead:
                        reached(dve, x_loaded, i + 1)
                        layer_norm_moments(i + 1, x_sb, bn_sb, moments, ln_bn, ln_moments)
                    if slot == AT["ln_scale"] and ahead:
                        reached(dve, ln_rstd, i + 1)
                        reached(dve, hT_filled, i)
                        layer_norm_scale(x_norm, x_sb, moments, rstd, ln_done)
                    if slot == AT["v"] and ahead:
                        reached(dve, v_filled, i + 1)
                        reached(dve, v_ready, i)
                        dve.tensor_tensor(v_stage[:, :, :], work_bank[:, :].rearrange("p (t d) -> p t d", t=T),
                                          bias_v[:, :].unsqueeze(1).broadcast_to([P, T, D]),
                                          ALU.add).then_inc(v_staged.sem, 1)
                    if slot == AT["y1"] and prev:
                        heads_out(i - 1, 1)
                    if slot in (AT["q"], AT["k"]) and ahead:
                        which = (AT["q"], AT["k"]).index(slot)
                        reached(dve, qk_filled, i + 1, which + 1)
                        reached(dve, hi_ready, i + 1, which + 1)
                        reached(dve, lo_ready, i, which + 1)
                        dve.scalar_tensor_tensor(resid[:, which, :], work_bank[:, :],
                                                 (bias_q, bias_k)[which][:, 0:1], split[:, which, 0, :],
                                                 ALU.add, ALU.subtract).then_inc(rest_ready.sem, 1)
                    if slot == AT["attn"] and prev:
                        reached(dve, attn_filled, i - 1)
                        reached(dve, x_resid_ready, i - 1)
                        reached(dve, x1_kept_ready, i - 2)
                        dve.tensor_tensor(x1[:, :, :], work_bank[:, :].rearrange("p (t d) -> p t d", t=T),
                                          x_resid[:, :, :], ALU.add).then_inc(x1_ready.sem, 1)
                    if slot == AT["ln2_moments"] and prev:
                        reached(dve, x1_ready, i - 1)
                        layer_norm_moments(i - 1, x1, bn2_sb, moments2, ln2_bn, ln2_moments)
                    if slot == AT["ln2_scale"] and prev:
                        reached(dve, ln2_rstd, i - 1)
                        reached(dve, h2T_filled, i - 2)
                        layer_norm_scale(x1_norm, x1, moments2, rstd2, ln2_done)
                    if slot == AT["z_sums"] and prev:
                        reached(dve, z_squared, i - 1)
                        reached(dve, rbf_bias_ready, i - 2)
                        dve.tensor_reduce(square_sum[:, :, :],
                                          z_square[:, :, :].rearrange("p t (a d) -> p t a d", a=2), AX_X,
                                          ALU.add).then_inc(sums_ready.sem, 1)
                    if slot == AT["y0"] and att:
                        heads_out(i, 0)

            iterations(dve, body)

        @block.scalar
        def _(act):
            act.wait_ge(s_loaded.sem, 11 * 16)
            act.wait_ge(s_masks.sem, 1)
            act.wait_ge(s_consts.sem, 1)

            def body(i, ahead, att, prev, old):
                for slot in range(SLOTS):
                    if att:
                        u = slot
                        reached(act, masked_ready, i, u + 1)
                        reached(act, turned, i, u - 3)
                        act.activation(probs[:, u % 4, :], masked[:, u % 4, :], ACT.Exp,
                                       bias=neg_max[:, u:u + 1], scale=-1.0).then_inc(probs_ready.sem, 1)
                    batch, u = lagged(i, slot, TURN_LAG)
                    if u not in VECTOR_UNITS and (att if slot >= TURN_LAG else prev):
                        reached(act, turned, batch, u + 1)
                        reached(act, pv_filled, batch - 1, u // (SLOTS // GROUPS) + 1)
                        h, t = divmod(u, T)
                        act.copy(probs_t[:, h // HG, h % HG, :, t * P:(t + 1) * P],
                                 turn_bank[u % 2][:, :].rearrange("p (j q) -> p j q", j=T)
                                 ).then_inc(copied_scalar.sem, 1)

                    if slot in AT["rbf_exp"] and old:
                        m = AT["rbf_exp"].index(slot)
                        reached(act, rbf_arg_ready, i - 2, m + 1)
                        if m == 0:
                            reached(act, rbf_bias_ready, i - 2)
                        if m >= 2:
                            reached(act, rbf_ready, i - 2, m - 1)
                        act.activation(rbf_exp[:, m % 2, :], rbf_arg[:, m % 2, :], ACT.Exp,
                                       bias=rbf_bias[:, m:m + 1]).then_inc(rbf_exp_ready.sem, 1)
                    if slot == AT["pv1_copy"] and prev:
                        reached(act, pv_filled, i - 1, 2)
                        reached(act, y_turned, i - 1, 1)
                        act.copy(pv_sb[:, :], pv_bank[:, :]).then_inc(pv_copied.sem, 1)
                    if slot == AT["hT"] and ahead:
                        reached(act, hT_filled, i + 1)
                        act.activation(hT[:, :], work_bank[:, :], ACT.Relu).then_inc(hT_ready.sem, 1)
                    if slot == AT["yT"] and prev:
                        reached(act, yT_filled, i - 1)
                        act.copy(yT[:, :], work_bank[:, :]).then_inc(yT_ready.sem, 1)
                    if slot in (AT["q"], AT["k"]) and ahead:
                        which = (AT["q"], AT["k"]).index(slot)
                        reached(act, qk_filled, i + 1, which + 1)
                        reached(act, split_stored, i, which + 1)
                        act.activation(split[:, which, 0, :], work_bank[:, :], ACT.Identity,
                                       bias=(bias_q, bias_k)[which][:, 0:1]).then_inc(hi_ready.sem, 1)
                    if slot == AT["h2T"] and prev:
                        reached(act, h2T_filled, i - 1)
                        act.activation(h2T[:, :], work_bank[:, :], ACT.Relu).then_inc(h2T_ready.sem, 1)
                    if slot in AT["z"] and prev:
                        t = AT["z"].index(slot)
                        reached(act, z_filled, i - 1, t + 1)
                        act.copy(z[:, t, 0:3 * D], adj_bank[t % 2][:, 0:3 * D]).then_inc(z_ready.sem, 1)
                    if slot == AT["zgT"] and prev:
                        reached(act, zgT_filled, i - 1)
                        act.copy(zgT[:, :], work_bank[:, :]).then_inc(zgT_ready.sem, 1)
                        act.activation(zgT_square[:, :], work_bank[:, :], ACT.Square
                                       ).then_inc(zgT_squared.sem, 1)
                    if slot == AT["pv0_copy"] and att:
                        reached(act, pv_filled, i, 1)
                        reached(act, y_turned, i - 1, 2)
                        act.copy(pv_sb[:, :], pv_bank[:, :]).then_inc(pv_copied.sem, 1)
                    if slot == AT["col"] and prev:
                        reached(act, col_filled, i - 1)
                        reached(act, rbf_arg_ready, i - 2)
                        act.copy(col_term[:, :], work_bank[:, :]).then_inc(col_ready.sem, 1)
                    if slot == AT["zlT"] and prev:
                        reached(act, zlT_filled, i - 1)
                        act.copy(zlT[:, :], work_bank[:, :]).then_inc(zlT_ready.sem, 1)

            iterations(act, body)


_INS = ["x", "adj", "L0_gnn_W_qkv", "L0_gnn_b_qkv", "L0_gnn_W_out", "L0_gnn_b_out",
        "L1_gnn_Wl", "L1_gnn_Wg", "L1_gnn_Wv", "L1_gnn_Wo"]
_OUTS = [((16, 512, 128), "float32")]


def kernel(**inputs):
    import numpy as _np
    import concourse.bacc as _bacc
    from concourse import mybir as _mybir
    from concourse.bass_utils import run_bass_kernel_spmd as _run

    nc = _bacc.Bacc("TRN2", target_bir_lowering=False, num_devices=1)
    arrays, args = {}, []
    for name in _INS:
        a = _np.ascontiguousarray(inputs[name])
        arrays[f"in_{name}_dram"] = a
        args.append(nc.dram_tensor(f"in_{name}_dram", a.shape, _mybir.dt.from_np(a.dtype), kind="ExternalInput").ap())
    for i, (shape, dtype) in enumerate(_OUTS):
        dt = _mybir.dt.from_np(_np.dtype(dtype))
        args.append(nc.dram_tensor(f"out_{i}_dram", shape, dt, kind="ExternalOutput").ap())
    graph_blocks(nc, *args)
    r = _run(nc, [arrays], core_ids=[0])
    got = tuple(r.results[0][f"out_{i}_dram"] for i in range(len(_OUTS)))
    return got[0]
```

```python
from contextlib import ExitStack

import concourse.bass as bass
from concourse import mybir

F32 = mybir.dt.float32
F32R = mybir.dt.float32r
BF16 = mybir.dt.bfloat16
ALU = mybir.AluOpType
ACT = mybir.ActivationFunctionType

P = 128
LN_EPS = 1e-5
KERNEL_EPS = 1e-8
W_LOCAL, W_GLOBAL = 0.9, 0.1
BIG = 2.0 ** 100
LEAST_SQUARE = KERNEL_EPS * KERNEL_EPS

Q_PARTS = (0, 0, 0, 1, 1, 2)
K_PARTS = (0, 1, 2, 0, 1, 0)

TURN_LAG = 3
VECTOR_UNITS = (3, 5, 6, 17, 21, 22, 27, 28)
AT = {
    "ln_moments": 0, "ln_rstd": 5, "ln_scale": 2, "hT": 3, "hT_split": 4, "q": 6, "k": 8, "v": 17,
    "v_move": 6, "rbf": (1, 3, 9, 13), "rbf_exp": (2, 4, 10, 13), "rbf_mask": (4, 6, 12, 15),
    "cos": (2, 9, 12, 14), "pv1": (3, 4, 5, 7), "pv1_copy": 7, "y1": 11, "yT": 12, "attn": 14,
    "mix_cos": (15, 16, 20, 22), "mix_rbf": (16, 18, 20, 22), "ln2_moments": 15, "ln2_rstd": 15,
    "ln2_scale": 18, "h2T": 20, "z": (22, 23, 24, 25), "z_sums": 26, "z_norms": 28, "zgT": 26, "col": 30,
    "zlT": 31, "pv0": (22, 26, 28, 29), "pv0_copy": 27, "y0": 29, "resid_move": 11, "x_biased": 16,
    "x1_keep": 29, "hT_read": 3, "v_read": 17, "y1_read": 11, "yT_read": 12, "attn_read": 14,
    "h2T_read": 20, "zgT_read": 27, "col_read": 30, "y0_read": 29, "zlT_read": 31,
    "cos_read": (3, 9, 12, 14), "rbf_read": (1, 3, 9, 13), "z_read": (22, 23, 24, 25),
    "mix_read": (16, 18, 20, 22), "qk_read": (6, 9),
}


class Signal:

    def __init__(self, sem, per, step):
        self.sem, self.per, self.step = sem, per, step


def reached(engine, signal, batch, nth=None):
    count = (batch * signal.per + (signal.per if nth is None else nth)) * signal.step
    if isinstance(count, int) and count <= 0:
        return
    engine.wait_ge(signal.sem, count)


def graph_blocks(nc, x, adj, w_qkv, b_qkv, w_out, b_out, w_l, w_g, w_v, w_o, out):
    B, N, D = x.shape
    H = 8
    DH = D // H
    T = N // P
    GROUPS = 2
    HG = H // GROUPS
    SLOTS = H * T
    ROWS = len(Q_PARTS) * DH
    HALF = H // 2
    SCALE = float(DH) ** -0.5
    ZC = 3 * D + 2
    assert D == P and T == 4 and HG * 32 == P

    copied_by_vector = [u for u in range(SLOTS) if u in VECTOR_UNITS]
    copied_by_scalar = [u for u in range(SLOTS) if u not in VECTOR_UNITS]

    with ExitStack() as ctx:
        def sb(name, shape, dt=F32):
            return ctx.enter_context(nc.sbuf_tensor(name, shape, dt))

        def bank(name):
            return ctx.enter_context(nc.psum_tensor(name, [P, 512], F32))

        def signal(name, per=1, step=1):
            return Signal(ctx.enter_context(nc.semaphore(name)), per, step)

        wqkv_sb = sb("wqkv_sb", [P, 3 * D])
        wz_sb = sb("wz_sb", [P, 3 * D])
        wout_sb = sb("wout_sb", [P, D])
        bias_q = sb("bias_q", [P, 1])
        bias_k = sb("bias_k", [P, 1])
        bias_v = sb("bias_v", [P, D])
        bias_out = sb("bias_out", [P, D])
        wqk_parts = sb("wqk_parts", [P, 2, 2 * D], F32R)
        wz_parts = sb("wz_parts", [P, 2, 3 * D], F32R)
        ident = sb("ident", [P, P])
        minus_half = sb("minus_half", [P, T])
        degree_floor = sb("degree_floor", [P, 2])
        mask_add = sb("mask_add", [P, T, N], BF16)
        mask_t = sb("mask_t", [P, T, N], BF16)

        x_sb = sb("x_sb", [P, T, D])
        bn_sb = sb("bn_sb", [P, T, 6])
        moments = sb("moments", [P, T, 2])
        var_eps = sb("var_eps", [P, T])
        rstd = sb("rstd", [P, T])
        x_norm = sb("x_norm", [P, T, D])
        x_biased = sb("x_biased", [P, T, D])
        x_resid = sb("x_resid", [P, T, D])
        hT = sb("hT", [P, N])
        hT_parts = sb("hT_parts", [P, 2, N], F32R)
        split = sb("split", [P, 2, 3, N], BF16)
        resid = sb("resid", [P, N])
        qk_rows = sb("qk_rows", [ROWS, 2, H, N], BF16)
        v_stage = sb("v_stage", [P, T, D])
        v_cols = sb("v_cols", [P, T, H, 32])
        masked = sb("masked", [P, 4, N])
        wv_sb = masked[:, 0, 0:D]
        wo_sb = masked[:, 0, D:2 * D]
        wvT_sb = masked[:, 0, 2 * D:3 * D]
        adj_sb = masked[:, 1, :].bitcast(adj.dtype).rearrange("p (t k) -> p t k", t=T)
        neg_max = sb("neg_max", [P, SLOTS])
        probs = sb("probs", [P, 4, N])
        probs_t = sb("probs_t", [P, GROUPS, HG, T, N])
        pv_sb = sb("pv_sb", [P, N])
        inv_den = sb("inv_den", [P, T, HG])
        y_sb = sb("y_sb", [P, T, D])
        yT = sb("yT", [P, N])

        x1 = sb("x1", [P, T, D])
        x1_kept = sb("x1_kept", [P, T, D])
        bn2_sb = sb("bn2_sb", [P, T, 6])
        moments2 = sb("moments2", [P, T, 2])
        var_eps2 = sb("var_eps2", [P, T])
        rstd2 = sb("rstd2", [P, T])
        x1_norm = sb("x1_norm", [P, T, D])
        h2T_parts = sb("h2T_parts", [P, 2, N], F32R)
        z = sb("z", [P, T, ZC])
        square_sum = sb("square_sum", [P, T, 2])
        norm_floor = sb("norm_floor", [P, T])
        inv_norm = sb("inv_norm", [P, T])
        rbf_bias = sb("rbf_bias", [P, T])
        zl_unit = sb("zl_unit", [P, T, D])
        zlT_parts = sb("zlT_parts", [P, 2, N], F32R)
        zgT_parts = sb("zgT_parts", [P, 2, N], F32R)
        col_term = sb("col_term", [P, N])
        rbf_arg = sb("rbf_arg", [P, 2, N])
        rbf_exp = sb("rbf_exp", [P, 2, N])
        adj_cos = sb("adj_cos", [P, T, N])
        adj_rbf = sb("adj_rbf", [P, T, N])
        z_square = adj_cos[:, 0:2 * D * T // N, :].rearrange("p a (t d) -> p (a t) d", d=2 * D)
        degree = sb("degree", [P, 2])
        inv_degree = sb("inv_degree", [P, 2])
        half_sum = sb("half_sum", [P, D])
        out_sb = sb("out_sb", [P, T, D])

        split_dram = nc.dram_tensor("split_dram", (2, 3, P, N), BF16, kind="Internal").ap()

        score_bank = [bank("score0"), bank("score1")]
        turn_bank = [bank("turn0"), bank("turn1")]
        pv_bank = bank("pv")
        work_bank = bank("work")
        adj_bank = [bank("adj0"), bank("adj1")]

        s_qkv_loaded = signal("setup_qkv_loaded", 5, 16)
        s_loaded = signal("setup_loaded", 6, 16)
        s_blank = signal("setup_blank")
        s_ident = signal("setup_ident")
        s_consts = signal("setup_consts")
        s_adj_cast = signal("setup_adj_cast")
        s_adj_open = signal("setup_adj_open")
        s_adj_turned = signal("setup_adj_turned", T)
        s_mask_add = signal("setup_mask_add")
        s_masks = signal("setup_masks")
        s_wv_turned = signal("setup_wv_turned")
        s_wv_copied = signal("setup_wv_copied")
        s_wvo = signal("setup_wvo")
        s_wvo_copied = signal("setup_wvo_copied")
        s_wqk_hi = signal("setup_wqk_hi")
        s_wqk_split = signal("setup_wqk_split")
        s_wz_hi = signal("setup_wz_hi")
        s_wz_split = signal("setup_wz_split")

        dve_steps = signal("dve_steps")
        pool_steps = signal("pool_steps")

        x_loaded = signal("x_loaded", 1, 16)
        ln_bn = signal("ln_bn")
        ln_moments = signal("ln_moments")
        ln_var = signal("ln_var")
        ln_rstd = signal("ln_rstd")
        ln_done = signal("ln_done")
        x_biased_ready = signal("x_biased_ready")
        x_resid_ready = signal("x_resid_ready")
        hT_filled = signal("hT_filled")
        hT_ready = signal("hT_ready")
        hT_hi = signal("hT_hi")
        hT_split = signal("hT_split")
        qk_filled = signal("qk_filled", 2)
        hi_ready = signal("hi_ready", 2)
        rest_ready = signal("rest_ready", 2)
        mid_ready = signal("mid_ready", 2)
        lo_ready = signal("lo_ready", 2)
        split_stored = signal("split_stored", 2, 16)
        rows_loaded = [signal(f"rows_loaded{h}", 2 * len(Q_PARTS), 16) for h in range(2)]

        v_filled = signal("v_filled")
        v_staged = signal("v_staged")
        v_ready = signal("v_ready")
        scores_filled = signal("scores_filled", SLOTS)
        masked_ready = signal("masked_ready", SLOTS)
        probs_ready = signal("probs_ready", SLOTS)
        turned = signal("turned", SLOTS)
        copied_vector = signal("copied_vector", len(copied_by_vector))
        copied_scalar = signal("copied_scalar", len(copied_by_scalar))
        pv_filled = signal("pv_filled", GROUPS)
        pv_copied = signal("pv_copied", GROUPS)
        y_turned = signal("y_turned", GROUPS)
        den_ready = signal("den_ready", GROUPS)
        y_ready = signal("y_ready", GROUPS)
        yT_filled = signal("yT_filled")
        yT_ready = signal("yT_ready")
        attn_filled = signal("attn_filled")
        x1_ready = signal("x1_ready")
        x1_kept_ready = signal("x1_kept_ready")

        ln2_bn = signal("ln2_bn")
        ln2_moments = signal("ln2_moments")
        ln2_var = signal("ln2_var")
        ln2_rstd = signal("ln2_rstd")
        ln2_done = signal("ln2_done")
        h2T_filled = signal("h2T_filled")
        h2T_hi = signal("h2T_hi")
        h2T_split = signal("h2T_split")
        z_filled = signal("z_filled", T)
        z_ready = signal("z_ready", T)
        sums_ready = signal("sums_ready")
        floor_ready = signal("floor_ready")
        rbf_bias_ready = signal("rbf_bias_ready")
        inv_norm_ready = signal("inv_norm_ready")
        unit_ready = signal("unit_ready")
        zgT_filled = signal("zgT_filled")
        zgT_hi = signal("zgT_hi")
        zgT_split = signal("zgT_split")
        col_filled = signal("col_filled")
        col_ready = signal("col_ready")
        zlT_filled = signal("zlT_filled")
        zlT_hi = signal("zlT_hi")
        zlT_split = signal("zlT_split")
        cos_filled = signal("cos_filled", T)
        cos_ready = signal("cos_ready", T)
        rbf_filled = signal("rbf_filled", T)
        rbf_arg_ready = signal("rbf_arg_ready", T)
        rbf_exp_ready = signal("rbf_exp_ready", T)
        rbf_ready = signal("rbf_ready", T)
        mix_filled = signal("mix_filled", T)
        degree_ready = signal("degree_ready", T)
        inv_degree_ready = signal("inv_degree_ready", T)
        half_ready = signal("half_ready", T)
        out_ready = signal("out_ready", T)
        out_stored = signal("out_stored", 1, 16)

        def step_over(engine, counter):
            engine.sem_inc(counter.sem, 1)

        def lagged(i, slot, lag):
            return (i, slot - lag) if slot >= lag else (i - 1, slot - lag + SLOTS)

        def copies_reached(engine, batch, last):
            by_vector = sum(u <= last for u in copied_by_vector)
            by_scalar = sum(u <= last for u in copied_by_scalar)
            if by_vector:
                reached(engine, copied_vector, batch, by_vector)
            if by_scalar:
                reached(engine, copied_scalar, batch, by_scalar)

        def iterations(engine, body, rest_of_setup):
            body(-1, True, False, False, False)
            rest_of_setup()
            for i in (0, 1, 2):
                body(i, i + 1 < B, 0 <= i, 1 <= i, 2 <= i)
            with engine.Fori(3, B - 2) as i:
                body(i, True, True, True, True)
            for i in (B - 2, B - 1, B, B + 1):
                body(i, i + 1 < B, i < B, i - 1 < B, True)

        WORK_USES = sorted(
            [("hT", hT_ready, 1, 1), ("q", rest_ready, 1, 1), ("k", rest_ready, 2, 1), ("v", v_staged, 1, 1),
             ("y1", y_ready, 2, -1), ("yT", yT_ready, 1, -1), ("attn", x1_ready, 1, -1),
             ("h2T", h2T_split, 1, -1), ("zgT", zgT_split, 1, -1), ("col", col_ready, 1, -1),
             ("y0", y_ready, 1, 0), ("zlT", zlT_split, 1, -1)], key=lambda use: AT[use[0]])

        def work_bank_free(engine, i, use):
            at = [name for name, _, _, _ in WORK_USES].index(use)
            for back in range(1, len(WORK_USES) + 1):
                _, sig, nth, offset = WORK_USES[(at - back) % len(WORK_USES)]
                batch = i + offset - (1 if back > at else 0)
                if isinstance(batch, int) and not 0 <= batch < B:
                    continue
                reached(engine, sig, batch, nth)
                return

        block = ctx.enter_context(nc.Block())

        @block.sync
        def _(sp):
            def load_x(batch):
                sp.dma_start(x_sb[:, :, :], x[batch].rearrange("(t p) d -> p t d", p=P)).then_inc(x_loaded.sem, 16)

            load_x(0)
            for dst, src in (
                (wqkv_sb[:, :], w_qkv),
                (bias_q[:, :], b_qkv[0:D].rearrange("(p o) -> p o", o=1)),
                (bias_k[:, :], b_qkv[D:2 * D].rearrange("(p o) -> p o", o=1)),
                (bias_v[:, :], b_qkv[2 * D:3 * D].partition_broadcast(P)),
                (bias_out[:, :], b_out.partition_broadcast(P)),
            ):
                sp.dma_start(dst, src).then_inc(s_qkv_loaded.sem, 16)
            for dst, src in (
                (adj_sb[:, :, :], adj.rearrange("(t p) k -> p t k", p=P)),
                (wout_sb[:, :], w_out),
                (wz_sb[:, 0:D], w_l),
                (wz_sb[:, D:2 * D], w_g),
                (wv_sb[:, :], w_v),
                (wo_sb[:, :], w_o),
            ):
                sp.dma_start(dst, src).then_inc(s_loaded.sem, 16)

            def load_rows(batch, half):
                h0 = half * HALF
                for which, parts in enumerate((Q_PARTS, K_PARTS)):
                    for block_row, part in enumerate(parts):
                        src = split_dram[which, part, h0 * DH:(h0 + HALF) * DH, :]
                        sp.dma_start(qk_rows[block_row * DH:(block_row + 1) * DH, which, h0:h0 + HALF, :],
                                     src.rearrange("(h f) n -> f h n", f=DH)).then_inc(rows_loaded[half].sem, 16)

            def body(i, ahead, att, prev, old):
                if ahead:
                    reached(sp, rows_loaded[0], i)
                    reached(sp, rows_loaded[1], i)
                    for which in range(2):
                        reached(sp, lo_ready, i + 1, which + 1)
                        reached(sp, hi_ready, i + 1, which + 1)
                        sp.dma_start(split_dram[which].rearrange("c f n -> f c n"),
                                     split[:, which, :, :]).then_inc(split_stored.sem, 16)
                    reached(sp, split_stored, i + 1)
                    reached(sp, scores_filled, i, SLOTS // 2)
                    load_rows(i + 1, 0)
                if old:
                    reached(sp, out_ready, i - 2)
                    sp.dma_start(out[i - 2].rearrange("(t p) d -> p t d", p=P),
                                 out_sb[:, :, :]).then_inc(out_stored.sem, 16)
                if ahead:
                    if not (isinstance(i, int) and i + 2 >= B):
                        reached(sp, ln_done, i + 1)
                        reached(sp, x_biased_ready, i + 1)
                        load_x(i + 2)
                    reached(sp, scores_filled, i, SLOTS)
                    load_rows(i + 1, 1)

            iterations(sp, body, lambda: None)
            reached(sp, out_stored, B - 1)
            reached(sp, split_stored, B - 1)

        @block.gpsimd
        def _(pool):
            pool.memset(ident[:, :], 0.0)
            pool.memset(minus_half[:, :], -0.5).then_inc(s_blank.sem, 1)
            pool.wait_ge(s_blank.sem, 1)
            pool.affine_select(out=ident[:, :], in_=ident[:, :], compare_op=ALU.not_equal, fill=1.0, base=0,
                               pattern=[[-1, P]], channel_multiplier=1).then_inc(s_ident.sem, 1)
            pool.wait_ge(s_qkv_loaded.sem, s_qkv_loaded.per * 16)

            def rest_of_setup():
                pool.memset(degree_floor[:, 0:1], KERNEL_EPS / W_LOCAL)
                pool.memset(degree_floor[:, 1:2], KERNEL_EPS / W_GLOBAL)
                pool.memset(z[:, :, 3 * D:3 * D + 1], 1.0 / W_LOCAL)
                pool.memset(z[:, :, 3 * D + 1:ZC], 1.0 / W_GLOBAL)
                pool.memset(v_cols[:, :, :, DH + 1:32], 0.0)
                pool.memset(v_cols[:, :, :, DH:DH + 1], 1.0).then_inc(s_consts.sem, 1)
                pool.wait_ge(s_adj_cast.sem, 1)
                pool.affine_select(out=probs[:, :, :], in_=probs[:, :, :], compare_op=ALU.not_equal, fill=0.0,
                                   base=0, pattern=[[P, T], [-1, N]],
                                   channel_multiplier=1).then_inc(s_adj_open.sem, 1)

            def body(i, ahead, att, prev, old):
                for slot in range(SLOTS):
                    if slot == AT["ln_rstd"] and ahead:
                        reached(pool, ln_moments, i + 1)
                        reached(pool, ln_done, i)
                        step_over(pool, pool_steps)
                        pool.tensor_scalar(var_eps[:, :], moments[:, :, 1], LN_EPS, None,
                                           ALU.add).then_inc(ln_var.sem, 1)
                        reached(pool, ln_var, i + 1)
                        pool.tensor_tensor(rstd[:, :], var_eps[:, :], minus_half[:, :],
                                           ALU.pow).then_inc(ln_rstd.sem, 1)
                    if slot in AT["qk_read"] and ahead:
                        which = AT["qk_read"].index(slot)
                        reached(pool, split_stored, i, which + 1)
                        reached(pool, rest_ready, i + 1, which + 1)
                        step_over(pool, pool_steps)
                        pool.tensor_copy(split[:, which, 1, :], resid[:, :]).then_inc(mid_ready.sem, 1)
                        reached(pool, mid_ready, i + 1, which + 1)
                        pool.tensor_tensor(split[:, which, 2, :], resid[:, :], split[:, which, 1, :],
                                           ALU.subtract).then_inc(lo_ready.sem, 1)
                    if slot == AT["v_move"] and att:
                        reached(pool, v_staged, i)
                        reached(pool, pv_filled, i - 1)
                        step_over(pool, pool_steps)
                        pool.tensor_copy(v_cols[:, :, :, 0:DH], v_stage[:, :, :].rearrange(
                            "p t (h c) -> p t h c", h=H)).then_inc(v_ready.sem, 1)
                    if slot == AT["ln2_rstd"] and prev:
                        reached(pool, ln2_moments, i - 1)
                        reached(pool, ln2_done, i - 2)
                        step_over(pool, pool_steps)
                        pool.tensor_scalar(var_eps2[:, :], moments2[:, :, 1], LN_EPS, None,
                                           ALU.add).then_inc(ln2_var.sem, 1)
                        reached(pool, ln2_var, i - 1)
                        pool.tensor_tensor(rstd2[:, :], var_eps2[:, :], minus_half[:, :],
                                           ALU.pow).then_inc(ln2_rstd.sem, 1)
                    if slot == AT["resid_move"] and att:
                        reached(pool, x1_ready, i - 1)
                        reached(pool, x_biased_ready, i)
                        step_over(pool, pool_steps)
                        pool.tensor_copy(x_resid[:, :, :], x_biased[:, :, :]).then_inc(x_resid_ready.sem, 1)
                    if slot == AT["x_biased"] and ahead:
                        reached(pool, x_loaded, i + 1)
                        reached(pool, x_resid_ready, i)
                        pool.tensor_tensor(x_biased[:, :, :], x_sb[:, :, :],
                                           bias_out[:, :].unsqueeze(1).broadcast_to([P, T, D]),
                                           ALU.add).then_inc(x_biased_ready.sem, 1)
                    if slot == AT["x1_keep"] and prev:
                        reached(pool, x1_ready, i - 1)
                        reached(pool, out_ready, i - 2)
                        step_over(pool, pool_steps)
                        pool.tensor_copy(x1_kept[:, :, :], x1[:, :, :]).then_inc(x1_kept_ready.sem, 1)
                    if slot == AT["z_norms"] and prev:
                        reached(pool, sums_ready, i - 1)
                        step_over(pool, pool_steps)
                        pool.tensor_scalar(norm_floor[:, :], square_sum[:, :, 0], LEAST_SQUARE, None,
                                           ALU.max).then_inc(floor_ready.sem, 1)
                        reached(pool, rbf_exp_ready, i - 2)
                        step_over(pool, pool_steps)
                        pool.tensor_scalar(rbf_bias[:, :], square_sum[:, :, 1], -0.5, None,
                                           ALU.mult).then_inc(rbf_bias_ready.sem, 1)
                        reached(pool, floor_ready, i - 1)
                        pool.tensor_tensor(inv_norm[:, :], norm_floor[:, :], minus_half[:, :],
                                           ALU.pow).then_inc(inv_norm_ready.sem, 1)
                        reached(pool, inv_norm_ready, i - 1)
                        reached(pool, zlT_filled, i - 2)
                        pool.tensor_tensor(zl_unit[:, :, :], z[:, :, 0:D],
                                           inv_norm[:, :].unsqueeze(2).broadcast_to([P, T, D]),
                                           ALU.mult).then_inc(unit_ready.sem, 1)

            iterations(pool, body, rest_of_setup)

        @block.tensor
        def _(pe):
            pe.wait_ge(s_ident.sem, 1)
            pe.wait_ge(s_qkv_loaded.sem, s_qkv_loaded.per * 16)
            pe.wait_ge(s_wqk_split.sem, 1)

            def rest_of_setup():
                pe.wait_ge(s_loaded.sem, s_loaded.per * 16)
                pe.transpose(adj_bank[0][:, 0:D], wv_sb[:, :], ident[:, :]).then_inc(s_wv_turned.sem, 1)
                pe.wait_ge(s_wv_copied.sem, 1)
                pe.matmul(adj_bank[1][:, 0:D], wvT_sb[:, :], wo_sb[:, :], start=True,
                          stop=True).then_inc(s_wvo.sem, 1)
                pe.wait_ge(s_adj_open.sem, 1)
                for m, dst in enumerate(score_bank + turn_bank):
                    for t in range(T):
                        last = pe.transpose(dst[:, t * P:(t + 1) * P], probs[:, t, m * P:(m + 1) * P],
                                            ident[:, :])
                    last.then_inc(s_adj_turned.sem, 1)
                pe.wait_ge(s_consts.sem, 1)
                pe.wait_ge(s_masks.sem, 1)
                pe.wait_ge(s_wz_split.sem, 1)

            def scores(batch, u):
                h, t = divmod(u, T)
                if u % (SLOTS // 2) == 0:
                    reached(pe, rows_loaded[u // (SLOTS // 2)], batch)
                reached(pe, masked_ready, batch, u - 1)
                pe.matmul(score_bank[u % 2][:, :], qk_rows[:, 0, h, t * P:(t + 1) * P], qk_rows[:, 1, h, :],
                          start=True, stop=True).then_inc(scores_filled.sem, 1)

            def turn(batch, u):
                reached(pe, probs_ready, batch, u + 1)
                if u >= 2:
                    copies_reached(pe, batch, u - 2)
                else:
                    copies_reached(pe, batch - 1, SLOTS + u - 2)
                for j in range(T):
                    last = pe.transpose(turn_bank[u % 2][:, j * P:(j + 1) * P],
                                        probs[:, u % 4, j * P:(j + 1) * P], ident[:, :])
                last.then_inc(turned.sem, 1)

            def attend(batch, group, j):
                if j == 0:
                    copies_reached(pe, batch, (group + 1) * SLOTS // GROUPS - 1)
                    reached(pe, v_ready, batch)
                    reached(pe, pv_copied, batch, group)
                for hl in range(HG):
                    last = pe.matmul(pv_bank[32 * hl:32 * (hl + 1), :], v_cols[:, j, group * HG + hl, :],
                                     probs_t[:, group, hl, j, :], start=(j == 0), stop=(j == T - 1),
                                     tile_position=(0, 32 * hl))
                if j == T - 1:
                    last.then_inc(pv_filled.sem, 1)

            def split_product(dst, left, right):
                for part, (a, b) in enumerate(((0, 0), (0, 1), (1, 0))):
                    last = pe.matmul(dst, left(a), right(b), start=(part == 0), stop=(part == 2))
                return last

            def mix(n, at, adjacency):
                for m in range(T):
                    last = pe.matmul(adj_bank[n % 2][:, at:at + D + 2], adjacency[:, m, n * P:(n + 1) * P],
                                     z[:, m, 2 * D:ZC], start=(m == 0), stop=(m == T - 1))
                return last

            def turn_tiles(src, ready):
                for t in range(T):
                    last = pe.transpose(work_bank[:, t * P:(t + 1) * P], src(t), ident[:, :])
                last.then_inc(ready.sem, 1)

            def body(i, ahead, att, prev, old):
                for slot in range(SLOTS):
                    if att:
                        scores(i, slot)
                    batch, u = lagged(i, slot, TURN_LAG)
                    if (att if slot >= TURN_LAG else prev):
                        turn(batch, u)

                    if slot in AT["cos"] and old:
                        m = AT["cos"].index(slot)
                        if m == 0:
                            reached(pe, zlT_split, i - 2)
                            reached(pe, z_ready, i - 2, T - 1)
                        else:
                            reached(pe, cos_ready, i - 2, m)
                        split_product(adj_bank[0][:, :], lambda a: zlT_parts[:, a, m * P:(m + 1) * P],
                                      lambda b: zlT_parts[:, b, :]).then_inc(cos_filled.sem, 1)
                    if slot in AT["rbf"] and old:
                        m = AT["rbf"].index(slot)
                        if m == 0:
                            reached(pe, zgT_split, i - 2)
                            reached(pe, z_ready, i - 2, T)
                        else:
                            reached(pe, rbf_arg_ready, i - 2, m)
                        split_product(adj_bank[1][:, :], lambda a: zgT_parts[:, a, m * P:(m + 1) * P],
                                      lambda b: zgT_parts[:, b, :]).then_inc(rbf_filled.sem, 1)
                    if slot in AT["mix_cos"] and old:
                        n = AT["mix_cos"].index(slot)
                        if n == 0:
                            reached(pe, cos_ready, i - 2)
                        elif n == 1:
                            reached(pe, rbf_arg_ready, i - 2)
                        else:
                            reached(pe, out_ready, i - 2, n - 1)
                        mix(n, 0, adj_cos)
                    if slot in AT["mix_rbf"] and old:
                        n = AT["mix_rbf"].index(slot)
                        if n == 0:
                            reached(pe, rbf_ready, i - 2)
                        mix(n, 256, adj_rbf).then_inc(mix_filled.sem, 1)

                    if slot in AT["pv1"] and prev:
                        attend(i - 1, 1, AT["pv1"].index(slot))
                    if slot in AT["pv0"] and att:
                        attend(i, 0, AT["pv0"].index(slot))

                    if slot == AT["hT"] and ahead:
                        reached(pe, ln_done, i + 1)
                        work_bank_free(pe, i, "hT")
                        turn_tiles(lambda t: x_norm[:, t, :], hT_filled)
                    if slot in (AT["q"], AT["k"]) and ahead:
                        which = (AT["q"], AT["k"]).index(slot)
                        reached(pe, hT_split, i + 1)
                        work_bank_free(pe, i, "qk"[which])
                        split_product(work_bank[:, :], lambda a: wqk_parts[:, a, which * D:(which + 1) * D],
                                      lambda b: hT_parts[:, b, :]).then_inc(qk_filled.sem, 1)
                    if slot == AT["v"] and ahead:
                        reached(pe, hT_ready, i + 1)
                        work_bank_free(pe, i, "v")
                        for t in range(T):
                            last = pe.matmul(work_bank[:, t * P:(t + 1) * P], hT[:, t * P:(t + 1) * P],
                                             wqkv_sb[:, 2 * D:3 * D], start=True, stop=True)
                        last.then_inc(v_filled.sem, 1)
                    if slot == AT["y1"] and prev:
                        reached(pe, pv_copied, i - 1, 2)
                        work_bank_free(pe, i, "y1")
                        turn_tiles(lambda t: pv_sb[:, t * P:(t + 1) * P], y_turned)
                    if slot == AT["yT"] and prev:
                        reached(pe, y_ready, i - 1, 2)
                        work_bank_free(pe, i, "yT")
                        turn_tiles(lambda t: y_sb[:, t, :], yT_filled)
                    if slot == AT["attn"] and prev:
                        reached(pe, yT_ready, i - 1)
                        work_bank_free(pe, i, "attn")
                        for t in range(T):
                            last = pe.matmul(work_bank[:, t * P:(t + 1) * P], yT[:, t * P:(t + 1) * P],
                                             wout_sb[:, :], start=True, stop=True)
                        last.then_inc(attn_filled.sem, 1)
                    if slot == AT["h2T"] and prev:
                        reached(pe, ln2_done, i - 1)
                        work_bank_free(pe, i, "h2T")
                        turn_tiles(lambda t: x1_norm[:, t, :], h2T_filled)
                    if slot in AT["z"] and prev:
                        t = AT["z"].index(slot)
                        reached(pe, h2T_split, i - 1)
                        if t < 2:
                            reached(pe, out_ready, i - 2, t + 3)
                        else:
                            reached(pe, z_ready, i - 1, t - 1)
                        split_product(adj_bank[t % 2][:, 0:3 * D],
                                      lambda a: h2T_parts[:, a, t * P:(t + 1) * P],
                                      lambda b: wz_parts[:, b, :]).then_inc(z_filled.sem, 1)
                    if slot == AT["zgT"] and prev:
                        reached(pe, z_ready, i - 1)
                        work_bank_free(pe, i, "zgT")
                        turn_tiles(lambda t: z[:, t, D:2 * D], zgT_filled)
                    if slot == AT["col"] and prev:
                        reached(pe, rbf_bias_ready, i - 1)
                        work_bank_free(pe, i, "col")
                        turn_tiles(lambda t: rbf_bias[:, t:t + 1].broadcast_to([P, P]), col_filled)
                    if slot == AT["y0"] and att:
                        reached(pe, pv_copied, i, 1)
                        work_bank_free(pe, i, "y0")
                        turn_tiles(lambda t: pv_sb[:, t * P:(t + 1) * P], y_turned)
                    if slot == AT["zlT"] and prev:
                        reached(pe, unit_ready, i - 1)
                        work_bank_free(pe, i, "zlT")
                        turn_tiles(lambda t: zl_unit[:, t, :], zlT_filled)

            iterations(pe, body, rest_of_setup)

        @block.vector
        def _(dve):
            dve.wait_ge(s_qkv_loaded.sem, s_qkv_loaded.per * 16)
            dve.tensor_copy(wqk_parts[:, 0, :], wqkv_sb[:, 0:2 * D]).then_inc(s_wqk_hi.sem, 1)
            dve.wait_ge(s_wqk_hi.sem, 1)
            dve.tensor_tensor(wqk_parts[:, 1, :], wqkv_sb[:, 0:2 * D], wqk_parts[:, 0, :].bitcast(F32),
                              ALU.subtract).then_inc(s_wqk_split.sem, 1)

            def rest_of_setup():
                dve.wait_ge(s_loaded.sem, s_loaded.per * 16)
                dve.tensor_copy(probs[:, :, :], adj_sb[:, :, :]).then_inc(s_adj_cast.sem, 1)
                dve.tensor_scalar(mask_add[:, :, :], adj_sb[:, :, :], BIG, -BIG, ALU.mult,
                                  ALU.add).then_inc(s_mask_add.sem, 1)
                dve.wait_ge(s_wv_turned.sem, 1)
                dve.tensor_copy(wvT_sb[:, :], adj_bank[0][:, 0:D]).then_inc(s_wv_copied.sem, 1)
                dve.wait_ge(s_wvo.sem, 1)
                dve.tensor_copy(wz_sb[:, 2 * D:3 * D], adj_bank[1][:, 0:D]).then_inc(s_wvo_copied.sem, 1)
                dve.wait_ge(s_wvo_copied.sem, 1)
                dve.tensor_copy(wz_parts[:, 0, :], wz_sb[:, :]).then_inc(s_wz_hi.sem, 1)
                dve.wait_ge(s_wz_hi.sem, 1)
                dve.tensor_tensor(wz_parts[:, 1, :], wz_sb[:, :], wz_parts[:, 0, :].bitcast(F32),
                                  ALU.subtract).then_inc(s_wz_split.sem, 1)
                for m, src in enumerate(score_bank + turn_bank):
                    dve.wait_ge(s_adj_turned.sem, m + 1)
                    last = dve.tensor_copy(mask_t[:, m, :], src[:, :])
                last.then_inc(s_masks.sem, 1)
                dve.wait_ge(s_consts.sem, 1)
                dve.wait_ge(s_mask_add.sem, 1)
                dve.wait_ge(s_masks.sem, 1)

            def layer_norm_moments(batch, src, bn, mv, bn_done, mv_done):
                for t in range(T):
                    last = dve.bn_stats(bn[:, t, :], src[:, t, :])
                last.then_inc(bn_done.sem, 1)
                reached(dve, bn_done, batch)
                step_over(dve, dve_steps)
                for t in range(T):
                    last = dve.bn_aggr(mv[:, t, :], bn[:, t, :])
                last.then_inc(mv_done.sem, 1)

            def layer_norm_scale(dst, src, mv, inv_std, done):
                for t in range(T):
                    last = dve.tensor_scalar(dst[:, t, :], src[:, t, :], mv[:, t, 0:1], inv_std[:, t:t + 1],
                                             ALU.subtract, ALU.mult)
                last.then_inc(done.sem, 1)

            def heads_out(batch, group):
                heads = work_bank[:, :].rearrange("p (t h c) -> p t h c", t=T, h=HG)
                reached(dve, y_turned, batch, group + 1)
                dve.reciprocal(inv_den[:, :, :], heads[:, :, :, DH]).then_inc(den_ready.sem, 1)
                reached(dve, den_ready, batch, group + 1)
                reached(dve, yT_filled, batch - 1)
                dst = y_sb[:, :, group * HG * DH:(group + 1) * HG * DH]
                dve.tensor_tensor(dst.rearrange("p t (h c) -> p t h c", h=HG), heads[:, :, :, 0:DH],
                                  inv_den[:, :, :].unsqueeze(3).broadcast_to([P, T, HG, DH]),
                                  ALU.mult).then_inc(y_ready.sem, 1)

            def body(i, ahead, att, prev, old):
                for slot in range(SLOTS):
                    if att:
                        u = slot
                        reached(dve, scores_filled, i, u + 1)
                        reached(dve, probs_ready, i, u - 3)
                        step_over(dve, dve_steps)
                        dve.tensor_tensor_reduce(masked[:, u % 4, :], score_bank[u % 2][:, :],
                                                 mask_add[:, u % T, :], -SCALE, 3.0e38, ALU.add, ALU.min,
                                                 neg_max[:, u:u + 1]).then_inc(masked_ready.sem, 1)
                    batch, u = lagged(i, slot, TURN_LAG)
                    if u in VECTOR_UNITS and (att if slot >= TURN_LAG else prev):
                        reached(dve, turned, batch, u + 1)
                        reached(dve, pv_filled, batch - 1, u // (SLOTS // GROUPS) + 1)
                        h, t = divmod(u, T)
                        dve.tensor_copy(probs_t[:, h // HG, h % HG, :, t * P:(t + 1) * P],
                                        turn_bank[u % 2][:, :].rearrange("p (j q) -> p j q", j=T)
                                        ).then_inc(copied_vector.sem, 1)

                    if slot in AT["cos_read"] and old:
                        m = AT["cos_read"].index(slot)
                        reached(dve, cos_filled, i - 2, m + 1)
                        dve.scalar_tensor_tensor(adj_cos[:, m, :], adj_bank[0][:, :], 0.0, mask_t[:, m, :],
                                                 ALU.max, ALU.mult).then_inc(cos_ready.sem, 1)
                    if slot in AT["rbf_read"] and old:
                        m = AT["rbf_read"].index(slot)
                        reached(dve, rbf_filled, i - 2, m + 1)
                        if m == 0:
                            reached(dve, col_ready, i - 2)
                        if m >= 2:
                            reached(dve, rbf_exp_ready, i - 2, m - 1)
                        dve.tensor_tensor(rbf_arg[:, m % 2, :], adj_bank[1][:, :], col_term[:, :],
                                          ALU.add).then_inc(rbf_arg_ready.sem, 1)
                    if slot in AT["rbf_mask"] and old:
                        m = AT["rbf_mask"].index(slot)
                        reached(dve, rbf_exp_ready, i - 2, m + 1)
                        dve.scalar_tensor_tensor(adj_rbf[:, m, :], rbf_exp[:, m % 2, :], 1.0, mask_t[:, m, :],
                                                 ALU.min, ALU.mult).then_inc(rbf_ready.sem, 1)
                    if slot in AT["mix_read"] and old:
                        n = AT["mix_read"].index(slot)
                        src = adj_bank[n % 2]
                        reached(dve, mix_filled, i - 2, n + 1)
                        dve.tensor_tensor(degree[:, :], src[:, D:D + 258:257], degree_floor[:, :],
                                          ALU.max).then_inc(degree_ready.sem, 1)
                        reached(dve, degree_ready, i - 2, n + 1)
                        dve.reciprocal(inv_degree[:, :], degree[:, :]).then_inc(inv_degree_ready.sem, 1)
                        reached(dve, inv_degree_ready, i - 2, n + 1)
                        if n == 0:
                            reached(dve, x1_kept_ready, i - 2)
                            reached(dve, out_stored, i - 3)
                        dve.scalar_tensor_tensor(half_sum[:, :], src[:, 256:256 + D], inv_degree[:, 1:2],
                                                 x1_kept[:, n, :], ALU.mult,
                                                 ALU.add).then_inc(half_ready.sem, 1)
                        reached(dve, half_ready, i - 2, n + 1)
                        dve.scalar_tensor_tensor(out_sb[:, n, :], src[:, 0:D], inv_degree[:, 0:1],
                                                 half_sum[:, :], ALU.mult, ALU.add).then_inc(out_ready.sem, 1)

                    if slot == AT["ln_moments"] and ahead:
                        reached(dve, x_loaded, i + 1)
                        layer_norm_moments(i + 1, x_sb, bn_sb, moments, ln_bn, ln_moments)
                    if slot == AT["ln_scale"] and ahead:
                        reached(dve, ln_rstd, i + 1)
                        reached(dve, hT_filled, i)
                        layer_norm_scale(x_norm, x_sb, moments, rstd, ln_done)
                    if slot == AT["hT_split"] and ahead:
                        reached(dve, hT_ready, i + 1)
                        dve.tensor_copy(hT_parts[:, 0, :], hT[:, :]).then_inc(hT_hi.sem, 1)
                        reached(dve, hT_hi, i + 1)
                        dve.tensor_tensor(hT_parts[:, 1, :], hT[:, :], hT_parts[:, 0, :].bitcast(F32),
                                          ALU.subtract).then_inc(hT_split.sem, 1)
                    if slot == AT["h2T_read"] and prev:
                        reached(dve, h2T_hi, i - 1)
                        dve.scalar_tensor_tensor(h2T_parts[:, 1, :], work_bank[:, :], 0.0,
                                                 h2T_parts[:, 0, :].bitcast(F32), ALU.max,
                                                 ALU.subtract).then_inc(h2T_split.sem, 1)
                    if slot == AT["zgT_read"] and prev:
                        reached(dve, zgT_hi, i - 1)
                        dve.tensor_tensor(zgT_parts[:, 1, :], work_bank[:, :],
                                          zgT_parts[:, 0, :].bitcast(F32),
                                          ALU.subtract).then_inc(zgT_split.sem, 1)
                    if slot == AT["zlT_read"] and prev:
                        reached(dve, zlT_hi, i - 1)
                        dve.tensor_tensor(zlT_parts[:, 1, :], work_bank[:, :],
                                          zlT_parts[:, 0, :].bitcast(F32),
                                          ALU.subtract).then_inc(zlT_split.sem, 1)
                    if slot == AT["v_read"] and ahead:
                        reached(dve, v_filled, i + 1)
                        reached(dve, v_ready, i)
                        dve.tensor_tensor(v_stage[:, :, :], work_bank[:, :].rearrange("p (t d) -> p t d", t=T),
                                          bias_v[:, :].unsqueeze(1).broadcast_to([P, T, D]),
                                          ALU.add).then_inc(v_staged.sem, 1)
                    if slot == AT["y1_read"] and prev:
                        heads_out(i - 1, 1)
                    if slot in AT["qk_read"] and ahead:
                        which = AT["qk_read"].index(slot)
                        reached(dve, qk_filled, i + 1, which + 1)
                        reached(dve, hi_ready, i + 1, which + 1)
                        reached(dve, lo_ready, i + 1, which)
                        dve.scalar_tensor_tensor(resid[:, :], work_bank[:, :],
                                                 (bias_q, bias_k)[which][:, 0:1], split[:, which, 0, :],
                                                 ALU.add, ALU.subtract).then_inc(rest_ready.sem, 1)
                    if slot == AT["attn_read"] and prev:
                        reached(dve, attn_filled, i - 1)
                        reached(dve, x_resid_ready, i - 1)
                        reached(dve, x1_kept_ready, i - 2)
                        dve.tensor_tensor(x1[:, :, :], work_bank[:, :].rearrange("p (t d) -> p t d", t=T),
                                          x_resid[:, :, :], ALU.add).then_inc(x1_ready.sem, 1)
                    if slot == AT["ln2_moments"] and prev:
                        reached(dve, x1_ready, i - 1)
                        layer_norm_moments(i - 1, x1, bn2_sb, moments2, ln2_bn, ln2_moments)
                    if slot == AT["ln2_scale"] and prev:
                        reached(dve, ln2_rstd, i - 1)
                        reached(dve, h2T_filled, i - 2)
                        layer_norm_scale(x1_norm, x1, moments2, rstd2, ln2_done)
                    if slot == AT["z_sums"] and prev:
                        reached(dve, z_ready, i - 1)
                        reached(dve, rbf_bias_ready, i - 2)
                        step_over(dve, dve_steps)
                        for t in range(T):
                            for a in range(2):
                                part = z[:, t, a * D:(a + 1) * D]
                                last = dve.tensor_tensor_reduce(z_square[:, t, a * D:(a + 1) * D], part, part,
                                                                1.0, 0.0, ALU.mult, ALU.add,
                                                                square_sum[:, t, a:a + 1])
                        last.then_inc(sums_ready.sem, 1)
                    if slot == AT["y0_read"] and att:
                        heads_out(i, 0)

            iterations(dve, body, rest_of_setup)

        @block.scalar
        def _(act):
            act.wait_ge(s_qkv_loaded.sem, s_qkv_loaded.per * 16)

            def rest_of_setup():
                act.wait_ge(s_masks.sem, 1)

            def body(i, ahead, att, prev, old):
                for slot in range(SLOTS):
                    batch, u = lagged(i, slot, TURN_LAG)
                    if u not in VECTOR_UNITS and (att if slot >= TURN_LAG else prev):
                        reached(act, turned, batch, u + 1)
                        reached(act, pv_filled, batch - 1, u // (SLOTS // GROUPS) + 1)
                        h, t = divmod(u, T)
                        act.copy(probs_t[:, h // HG, h % HG, :, t * P:(t + 1) * P],
                                 turn_bank[u % 2][:, :].rearrange("p (j q) -> p j q", j=T)
                                 ).then_inc(copied_scalar.sem, 1)
                    if att:
                        u = slot
                        reached(act, masked_ready, i, u + 1)
                        reached(act, turned, i, u - 3)
                        act.activation(probs[:, u % 4, :], masked[:, u % 4, :], ACT.Exp,
                                       bias=neg_max[:, u:u + 1], scale=-1.0).then_inc(probs_ready.sem, 1)

                    if slot in AT["rbf_exp"] and old:
                        m = AT["rbf_exp"].index(slot)
                        reached(act, rbf_arg_ready, i - 2, m + 1)
                        if m == 0:
                            reached(act, rbf_bias_ready, i - 2)
                        if m >= 2:
                            reached(act, rbf_ready, i - 2, m - 1)
                        act.activation(rbf_exp[:, m % 2, :], rbf_arg[:, m % 2, :], ACT.Exp,
                                       bias=rbf_bias[:, m:m + 1]).then_inc(rbf_exp_ready.sem, 1)
                    if slot == AT["pv1_copy"] and prev:
                        reached(act, pv_filled, i - 1, 2)
                        reached(act, y_turned, i - 1, 1)
                        act.copy(pv_sb[:, :], pv_bank[:, :]).then_inc(pv_copied.sem, 1)
                    if slot == AT["hT_read"] and ahead:
                        reached(act, hT_filled, i + 1)
                        act.activation(hT[:, :], work_bank[:, :], ACT.Relu).then_inc(hT_ready.sem, 1)
                    if slot == AT["yT_read"] and prev:
                        reached(act, yT_filled, i - 1)
                        act.copy(yT[:, :], work_bank[:, :]).then_inc(yT_ready.sem, 1)
                    if slot in AT["qk_read"] and ahead:
                        which = AT["qk_read"].index(slot)
                        reached(act, qk_filled, i + 1, which + 1)
                        reached(act, split_stored, i, which + 1)
                        act.activation(split[:, which, 0, :], work_bank[:, :], ACT.Identity,
                                       bias=(bias_q, bias_k)[which][:, 0:1]).then_inc(hi_ready.sem, 1)
                    if slot == AT["h2T_read"] and prev:
                        reached(act, h2T_filled, i - 1)
                        act.activation(h2T_parts[:, 0, :], work_bank[:, :], ACT.Relu).then_inc(h2T_hi.sem, 1)
                    if slot in AT["z_read"] and prev:
                        t = AT["z_read"].index(slot)
                        reached(act, z_filled, i - 1, t + 1)
                        act.copy(z[:, t, 0:3 * D], adj_bank[t % 2][:, 0:3 * D]).then_inc(z_ready.sem, 1)
                    if slot == AT["zgT_read"] and prev:
                        reached(act, zgT_filled, i - 1)
                        act.copy(zgT_parts[:, 0, :], work_bank[:, :]).then_inc(zgT_hi.sem, 1)
                    if slot == AT["pv0_copy"] and att:
                        reached(act, pv_filled, i, 1)
                        reached(act, y_turned, i - 1, 2)
                        act.copy(pv_sb[:, :], pv_bank[:, :]).then_inc(pv_copied.sem, 1)
                    if slot == AT["col_read"] and prev:
                        reached(act, col_filled, i - 1)
                        reached(act, rbf_arg_ready, i - 2)
                        act.copy(col_term[:, :], work_bank[:, :]).then_inc(col_ready.sem, 1)
                    if slot == AT["zlT_read"] and prev:
                        reached(act, zlT_filled, i - 1)
                        act.copy(zlT_parts[:, 0, :], work_bank[:, :]).then_inc(zlT_hi.sem, 1)

            iterations(act, body, rest_of_setup)


_INS = ["x", "adj", "L0_gnn_W_qkv", "L0_gnn_b_qkv", "L0_gnn_W_out", "L0_gnn_b_out",
        "L1_gnn_Wl", "L1_gnn_Wg", "L1_gnn_Wv", "L1_gnn_Wo"]
_OUTS = [((16, 512, 128), "float32")]


def kernel(**inputs):
    import numpy as _np
    import concourse.bacc as _bacc
    from concourse import mybir as _mybir
    from concourse.bass_utils import run_bass_kernel_spmd as _run

    nc = _bacc.Bacc("TRN2", target_bir_lowering=False, num_devices=1)
    arrays, args = {}, []
    for name in _INS:
        a = _np.ascontiguousarray(inputs[name])
        arrays[f"in_{name}_dram"] = a
        args.append(nc.dram_tensor(f"in_{name}_dram", a.shape, _mybir.dt.from_np(a.dtype), kind="ExternalInput").ap())
    for i, (shape, dtype) in enumerate(_OUTS):
        dt = _mybir.dt.from_np(_np.dtype(dtype))
        args.append(nc.dram_tensor(f"out_{i}_dram", shape, dt, kind="ExternalOutput").ap())
    graph_blocks(nc, *args)
    r = _run(nc, [arrays], core_ids=[0])
    got = tuple(r.results[0][f"out_{i}_dram"] for i in range(len(_OUTS)))
    return got[0]
```
